# Optimizing a Trainium2 kernel written in Bass

```python
import numpy as np
import jax
import jax.numpy as jnp

def _softmax(x, axis=-1):
    return jax.nn.softmax(x, axis=axis)

def _gelu(x):
    return jax.nn.gelu(x, approximate=True)

def _silu(x):
    return jax.nn.silu(x)

def _sigmoid(x):
    return jax.nn.sigmoid(x)

def _layernorm(x, axis=-1, eps=1e-05):
    m = jnp.mean(x, axis=axis, keepdims=True)
    v = jnp.var(x, axis=axis, keepdims=True)
    return (x - m) / jnp.sqrt(v + eps)

def _scatter_add(tgt, idx, src, axis=0):
    return tgt.at[idx].add(src)

def _segment_sum(src, seg, n):
    return jax.ops.segment_sum(src, seg, n)
kernel_name = 'mk_flamingo_gated_d1_seqx_r4_0fe455'

def setup_inputs(seed: int=0):
    np.random.seed(seed)
    _w = jnp.asarray

    def _rec_inputs():
        import jax
        import jax.numpy as jnp
        _rk = jax.random.key(seed)
        x = 7.22e-05 + 1 * jax.random.normal(jax.random.fold_in(_rk, 1), (16, 128, 512), jnp.float32)
        _lenS = 128 - jax.random.randint(jax.random.fold_in(_rk, 7), (16,), 0, max(1, 128 // 4) + 1, jnp.int32)
        _lenS2 = 128 - jax.random.randint(jax.random.fold_in(_rk, 8), (16,), 0, max(1, 128 // 4) + 1, jnp.int32)
        _ctx_2048P = jax.random.normal(jax.random.fold_in(_rk, 11), (16, 16, 512), jnp.float32)
        _ctx_2048c = jax.random.dirichlet(jax.random.fold_in(_rk, 511), 0.3 * jnp.ones((16,), jnp.float32), (16, 128))
        _ctx_2048t = jnp.einsum('bsk,bkd->bsd', _ctx_2048c, _ctx_2048P)
        _ctx_2048t = _ctx_2048t * jax.lax.rsqrt(jnp.mean(jnp.square(_ctx_2048t)) + 1e-12) * 0.953939
        ctx_2048 = 4.13588e-05 + 0.999923 * (_ctx_2048t + 0.3 * jax.random.normal(jax.random.fold_in(_rk, 611), (16, 128, 512), jnp.float32))
        _g = jax.random.normal(jax.random.fold_in(_rk, 9001), (2, 1), jnp.float32)
        _g = jnp.sign(_g) * jnp.maximum(jnp.abs(_g), 1.0) + (_g == 0) * 1.0
        g_xattn = _g[0]
        g_ffn = _g[1]
        return (x, ctx_2048, g_xattn, g_ffn)
    x, ctx_2048, g_xattn, g_ffn = _rec_inputs()

    def _L0_xattn_setup():
        import jax, jax.numpy as jnp
        import numpy as np
        B, S, DIM, HD = (4, 256, 512, 128)
        H = DIM // HD
        GN_EPS = 0.001

        def _decay_masks(n_heads, seq_len):
            gam = 1.0 - 2.0 ** (-5.0 - jnp.arange(n_heads, dtype=jnp.float32))
            idx = jnp.arange(seq_len, dtype=jnp.float32)
            expo = idx[None, :] - idx[:, None]
            D = jnp.where(expo[None, :, :] <= 0, gam[:, None, None] ** expo[None, :, :], 0.0)
            return D / jnp.sqrt(D.sum(axis=-1))[:, None, :]
        key = jax.random.key(seed)
        ks = jax.random.split(key, 8)
        x = jax.random.normal(ks[0], (B, S, DIM), dtype=jnp.float32)
        k = jax.random.normal(ks[1], (B, S, DIM), dtype=jnp.float32)
        v = jax.random.normal(ks[2], (B, S, DIM), dtype=jnp.float32)
        Wh = jax.random.normal(ks[3], (H, HD, HD), dtype=jnp.float32) / np.sqrt(HD)
        wg_w = jax.random.normal(ks[4], (DIM, DIM), dtype=jnp.float32) / np.sqrt(DIM)
        wo_w = jax.random.normal(ks[5], (DIM, DIM), dtype=jnp.float32) / np.sqrt(DIM)
        gn_gamma = jnp.ones((DIM,), dtype=jnp.float32)
        gn_beta = jnp.zeros((DIM,), dtype=jnp.float32)
        return {'x': x, 'k': k, 'v': v, 'Wh': Wh, 'wg_w': wg_w, 'wo_w': wo_w, 'gn_gamma': gn_gamma, 'gn_beta': gn_beta}
    _L0_xattn_all = _L0_xattn_setup()
    _L0_xattn_in = {k: v for k, v in _L0_xattn_all.items() if k in ('Wh', 'wg_w', 'wo_w', 'gn_gamma', 'gn_beta')}
    del _L0_xattn_all

    def _L0_ffn_setup():
        import jax, jax.numpy as jnp
        import numpy as np
        HIDDEN = 512
        INTER = 1408
        B, S = (2, 512)

        def _ternary(key, shape):
            return jax.random.randint(key, shape, -1, 2).astype(jnp.float32)
        key = jax.random.key(seed)
        ks = jax.random.split(key, 7)
        x = jax.random.normal(ks[0], (B, S, HIDDEN), dtype=jnp.float32)
        gate_w = _ternary(ks[1], (INTER, HIDDEN))
        up_w = _ternary(ks[2], (INTER, HIDDEN))
        down_w = _ternary(ks[3], (HIDDEN, INTER))
        gate_s = jax.random.uniform(ks[4], (INTER,), minval=0.01, maxval=0.1, dtype=jnp.float32)
        up_s = jax.random.uniform(ks[5], (INTER,), minval=0.01, maxval=0.1, dtype=jnp.float32)
        down_s = jax.random.uniform(ks[6], (HIDDEN,), minval=0.01, maxval=0.1, dtype=jnp.float32)
        return {'x': x, 'gate_w': gate_w, 'up_w': up_w, 'down_w': down_w, 'gate_s': gate_s, 'up_s': up_s, 'down_s': down_s}
    _L0_ffn_all = _L0_ffn_setup()
    _L0_ffn_in = {k: v for k, v in _L0_ffn_all.items() if k in ('gate_w', 'up_w', 'down_w', 'gate_s', 'up_s', 'down_s')}
    del _L0_ffn_all
    return {'x': x, 'ctx_2048': ctx_2048, 'g_xattn': g_xattn, 'g_ffn': g_ffn, 'L0_xattn_Wh': _L0_xattn_in['Wh'], 'L0_xattn_wg_w': _L0_xattn_in['wg_w'], 'L0_xattn_wo_w': _L0_xattn_in['wo_w'], 'L0_xattn_gn_gamma': _L0_xattn_in['gn_gamma'], 'L0_xattn_gn_beta': _L0_xattn_in['gn_beta'], 'L0_ffn_gate_w': _L0_ffn_in['gate_w'], 'L0_ffn_up_w': _L0_ffn_in['up_w'], 'L0_ffn_down_w': _L0_ffn_in['down_w'], 'L0_ffn_gate_s': _L0_ffn_in['gate_s'], 'L0_ffn_up_s': _L0_ffn_in['up_s'], 'L0_ffn_down_s': _L0_ffn_in['down_s']}

def reference(x, ctx_2048, g_xattn, g_ffn, L0_xattn_Wh, L0_xattn_wg_w, L0_xattn_wo_w, L0_xattn_gn_gamma, L0_xattn_gn_beta, L0_ffn_gate_w, L0_ffn_up_w, L0_ffn_down_w, L0_ffn_gate_s, L0_ffn_up_s, L0_ffn_down_s):
    import jax
    import jax.numpy as jnp

    def _L0_xattn_ref(x, k, v, Wh, wg_w, wo_w, gn_gamma, gn_beta):
        import jax, jax.numpy as jnp
        import numpy as np
        B, S, DIM, HD = (4, 256, 512, 128)
        H = DIM // HD
        GN_EPS = 0.001

        def _decay_masks(n_heads, seq_len):
            gam = 1.0 - 2.0 ** (-5.0 - jnp.arange(n_heads, dtype=jnp.float32))
            idx = jnp.arange(seq_len, dtype=jnp.float32)
            expo = idx[None, :] - idx[:, None]
            D = jnp.where(expo[None, :, :] <= 0, gam[:, None, None] ** expo[None, :, :], 0.0)
            return D / jnp.sqrt(D.sum(axis=-1))[:, None, :]
        b, s, dim = x.shape
        h, hd, _ = Wh.shape
        xh = x.reshape(b, s, h, hd)
        kh = k.reshape(b, s, h, hd)
        vh = v.reshape(b, s, h, hd)
        Q = jnp.einsum('bshd,hde->bshe', xh, Wh)
        K = jnp.einsum('bshd,hde->bshe', kh, Wh)
        V = jnp.einsum('bshd,hde->bshe', vh, Wh)
        scores = jnp.einsum('bshe,bthe->bhst', Q, K) / jnp.sqrt(jnp.float32(hd))
        Dn = _decay_masks(h, s)
        masked = scores * Dn[None, :, :, :]
        A = jnp.maximum(jnp.abs(masked.sum(axis=0)), 1.0)
        O = jnp.einsum('hst,bthe->bshe', A, V).reshape(b, s, dim)
        mu = O.mean(axis=-1, keepdims=True)
        var = O.var(axis=-1, keepdims=True)
        Y = (O - mu) / jnp.sqrt(var + GN_EPS) * gn_gamma + gn_beta
        W = jax.nn.relu(x @ wg_w)
        return W * Y @ wo_w

    def _L0_ffn_ref(x, gate_w, up_w, down_w, gate_s, up_s, down_s):
        import jax, jax.numpy as jnp
        import numpy as np
        HIDDEN = 512
        INTER = 1408
        B, S = (2, 512)

        def _ternary(key, shape):
            return jax.random.randint(key, shape, -1, 2).astype(jnp.float32)
        b, s, h = x.shape
        xf = x.reshape(b * s, h)
        g = jnp.einsum('th,ih->ti', xf, gate_w) * gate_s
        u = jnp.einsum('th,ih->ti', xf, up_w) * up_s
        hdn = jax.nn.silu(g) * u
        out = jnp.einsum('ti,hi->th', hdn, down_w) * down_s
        return out.reshape(b, s, -1)
    x = x + jnp.tanh(g_xattn[0]) * _L0_xattn_ref(_layernorm(x, axis=-1), ctx_2048, ctx_2048, L0_xattn_Wh, L0_xattn_wg_w, L0_xattn_wo_w, L0_xattn_gn_gamma, L0_xattn_gn_beta)
    x = x + jnp.tanh(g_ffn[0]) * _L0_ffn_ref(_layernorm(x, axis=-1), L0_ffn_gate_w, L0_ffn_up_w, L0_ffn_down_w, L0_ffn_gate_s, L0_ffn_up_s, L0_ffn_down_s)
    return x

_drawn_inputs = setup_inputs


def setup_inputs(seed=0):
    import zlib

    import numpy as np

    out = dict(_drawn_inputs(seed))
    spreads = {'L0_xattn_gn_gamma': (1.0, 0.2), 'L0_xattn_gn_beta': (0.0, 0.1)}
    factors = {}
    for name, (base, spread) in spreads.items():
        noise = np.random.default_rng([zlib.crc32(name.encode()), seed]).standard_normal(out[name].shape)
        drawn = base * np.exp(spread * noise) if base else spread * noise
        out[name] = jnp.asarray(drawn.astype(out[name].dtype))
    for name, factor in factors.items():
        out[name] = (out[name] * factor).astype(out[name].dtype)
    return out
```

```python
from contextlib import ExitStack

import numpy as np

import concourse.bass as bass
from concourse import mybir

F32 = mybir.dt.float32
F32R = mybir.dt.float32r
ALU = mybir.AluOpType
ACT = mybir.ActivationFunctionType

P = 128
B, S, D = 16, 128, 512
H = D // P
INTER = 1408
CH = INTER // P
GB = 4
GROUPS = B // GB
NT = GB * S
LN_EPS = 1e-5
GN_EPS = 1e-3

S_BANK = 0
T_BANKS = (1, 2)
X_BANKS = (3, 4)
V_BANKS = (5, 6)
W_BANKS = (7, 5, 6, 7)
O_BANK0 = 1
Z_BANKS = (5, 6)
WO_BANKS = (7, 0)
GU_BANKS = ((5, 6), (7, 0))

GS0, US0, GAM0, BET0, TG0 = 0, CH, 2 * CH, 2 * CH + H, 2 * CH + 2 * H
N_SMALL = TG0 + 2
WROW = 3 * D
LOW_CHUNKS = 6
EARLY_CHUNKS = 4

KB = 1024


def build(nc, x, ctxT, WhT, Wh, wg, wo, wffn, smalls, down_s, mask, out):
    base = -(-nc.sbuf_base // 64) * 64
    with ExitStack() as ctx:
        def at(name, offset, shape, dt=F32):
            return nc.alloc_sbuf_tensor_at(name, [P] + shape, dt, offset=base + int(offset))

        def sem(name):
            return ctx.enter_context(nc.semaphore(name))

        x_sb = at("x_sb", 0, [B, D])
        v_sb = at("v_sb", 32 * KB, [H, B, P])
        wT_sb = at("wT_sb", 64 * KB, [H, B * S])
        ctx_sb = at("ctx_sb", 96 * KB, [H, NT])
        t_sb = at("t_sb", 112 * KB, [H, NT])
        xT_sb = at("xT_sb", 120 * KB, [H, GB, S])
        xTh_sb = at("xTh_sb", 128 * KB, [H, GB, S], F32R)
        xTl_sb = at("xTl_sb", 136 * KB, [H, GB, S], F32R)
        wg_hi = at("wg_hi", 144 * KB, [H, D], F32R)
        wg_raw = at("wg_raw", 152 * KB, [H, D])
        wg_lo = at("wg_lo", 152 * KB, [H, D], F32R)
        wh_sb = at("wh_sb", 160 * KB, [H, P])
        whT_sb = at("whT_sb", 162 * KB, [H, P])
        g_sb = at("g_sb", 164 * KB, [H, P])
        mask_sb = at("mask_sb", 166 * KB, [H, P])
        wy_hi = at("wy_hi", 144 * KB, [H, GB, S], F32R)
        wy_lo = at("wy_lo", 152 * KB, [H, GB, S], F32R)
        x2n0_sb = at("x2n0_sb", 160 * KB, [GB, D])
        w_low = at("w_low", 96 * KB, [LOW_CHUNKS, 2, WROW], F32R)
        w_low_raw = at("w_low_raw", 96 * KB, [LOW_CHUNKS, 2, WROW])
        w_high = at("w_high", 32 * KB, [CH - LOW_CHUNKS, 2, WROW], F32R)
        w_high_raw = at("w_high_raw", 32 * KB, [CH - LOW_CHUNKS, 2, WROW])
        silu_sb = at("silu_sb", 92 * KB, [2, NT])
        wo_hi = at("wo_hi", 168 * KB, [H, D], F32R)
        wo_raw = at("wo_raw", 176 * KB, [H, D])
        wo_lo = at("wo_lo", 176 * KB, [H, D], F32R)
        hd_sb = at("hd_sb", 168 * KB, [2, 2, NT], F32R)
        x2n_sb = at("x2n_sb", 176 * KB, [GB, D])
        z_sb = at("z_sb", 184 * KB, [GB, D])
        x2h_sb = at("x2h_sb", 184 * KB, [H, GB, S], F32R)
        x2l_sb = at("x2l_sb", 192 * KB, [H, GB, S], F32R)
        top = 200 * KB
        aT_sb = at("aT_sb", top, [H, P])
        dsg_sb = at("dsg_sb", top + 2 * KB, [D])
        ident = at("ident", top + 4 * KB, [P])
        zero_sb = at("zero_sb", top + 4.5 * KB, [P])
        small = at("small", top + 5 * KB, [N_SMALL])
        tg = at("tg", top + 5.25 * KB, [2])
        eps = at("eps", top + 5.3125 * KB, [2])
        st6 = at("st6", top + 5.375 * KB, [GB, 6])
        mv = at("mv", top + 5.5 * KB, [GB, 2])
        std = at("std", top + 5.5625 * KB, [GB])
        rstd = at("rstd", top + 5.625 * KB, [GB])
        l_st6 = at("l_st6", top + 5.75 * KB, [GB, 6])
        l_mv = at("l_mv", top + 5.875 * KB, [GB, 2])
        mean2 = at("mean2", top + 5.9375 * KB, [B])
        std2 = at("std2", top + 6 * KB, [B])
        carrier = at("carrier", top + 6.1875 * KB, [1])
        rstd2 = at("rstd2", top + 6.125 * KB, [B])

        ps = ctx.enter_context(nc.psum_tensor("ps", [P, 8, 512], F32))

        whT_in, wh_in, small_in, mask_in = sem("whT_in"), sem("wh_in"), sem("small_in"), sem("mask_in")
        wg_in, wo_in = sem("wg_in"), sem("wo_in")
        x_in, ctx_in = sem("x_in"), sem("ctx_in")
        wffn_in = sem("wffn_in")
        ident_ok, zero_ok, eps_ok = sem("ident_ok"), sem("zero_ok"), sem("eps_ok")
        id0 = sem("id0")
        wg_ok, wo_ok = sem("wg_ok"), sem("wo_ok")
        wffn_hi, wffn_ok = sem("wffn_hi"), sem("wffn_ok")
        tanh_ok, dsg_ok = sem("tanh_ok"), sem("dsg_ok")
        g_mm, g_ok = sem("g_mm"), sem("g_ok")
        st_ok, mv_ok = sem("st_ok"), sem("mv_ok")
        std_ok, rstd_ok = sem("std_ok"), sem("rstd_ok")
        xn_ok, xt_mm = sem("xn_ok"), sem("xt_mm")
        xt_full, xt_hi, xt_lo = sem("xt_full"), sem("xt_hi"), sem("xt_lo")
        t_mm, t_ok = sem("t_mm"), sem("t_ok")
        v_mm, v_ok = sem("v_mm"), sem("v_ok")
        s_mm = sem("s_mm")
        w_mm, w_ok = sem("w_mm"), sem("w_ok")
        am_ok, a_ok = sem("am_ok"), sem("a_ok")
        o_mm, z_ok = sem("o_mm"), sem("z_ok")
        zt_mm, y_ok, wy_ok, wyh_ok, wyl_ok = (
            sem("zt_mm"), sem("y_ok"), sem("wy_ok"), sem("wyh_ok"), sem("wyl_ok"))
        wo_mm, x2_ok = sem("wo_mm"), sem("x2_ok")
        lst_ok, mv2_ok = sem("lst_ok"), sem("mv2_ok")
        std2_ok, rstd2_ok, mean2_ok = sem("std2_ok"), sem("rstd2_ok"), sem("mean2_ok")
        x2n_ok, x2t_mm, x2h_ok, x2l_ok = (
            sem("x2n_ok"), sem("x2t_mm"), sem("x2h_ok"), sem("x2l_ok"))
        gate_mm, up_mm, silu_ok = sem("gate_mm"), sem("up_mm"), sem("silu_ok")
        hd_ok, hdh_ok, hdl_ok, down_mm = sem("hd_ok"), sem("hdh_ok"), sem("hdl_ok"), sem("down_mm")
        acc_mm, sc_ok, fin_ok = sem("acc_mm"), sem("sc_ok"), sem("fin_ok")
        stored = sem("stored")

        def bank(i):
            return ps[:, i, :]

        def tiles(g):
            return bass.ds(g * GB, GB)

        def tokens(g):
            return bass.ds(g * NT, NT)

        def chunk_w(c, part):
            return w_low[:, c, part, :] if c < LOW_CHUNKS else w_high[:, c - LOW_CHUNKS, part, :]

        block = ctx.enter_context(nc.Block())

        @block.sync
        def _(sp):
            sp.dma_start(whT_sb[:], WhT).then_inc(whT_in, 16)
            sp.dma_start(x_sb[:, 0:GB, :], x[0:GB].rearrange("b s d -> s b d")).then_inc(x_in, 16)
            sp.dma_start(ctx_sb[:], ctxT[0]).then_inc(ctx_in, 16)
            sp.dma_start(small[:], smalls).then_inc(small_in, 16)
            sp.dma_start(dsg_sb[:], down_s.to_broadcast([P, D])).then_inc(small_in, 16)
            sp.dma_start(wh_sb[:], Wh).then_inc(wh_in, 16)
            sp.dma_start(wg_raw[:], wg).then_inc(wg_in, 16)
            sp.dma_start(wo_raw[:], wo).then_inc(wo_in, 16)
            sp.dma_start(mask_sb[:], mask).then_inc(mask_in, 16)
            with sp.Fori(1, GROUPS) as g:
                sp.wait_ge(x_in, 16 * g)
                sp.dma_start(x_sb[:, tiles(g), :],
                             x[tiles(g)].rearrange("b s d -> s b d")).then_inc(x_in, 16)
                sp.wait_ge(ctx_in, 16 * g)
                sp.wait_ge(v_mm, GB * g)
                sp.dma_start(ctx_sb[:], ctxT[bass.ds(g, 1)].rearrange("g p h n -> (g p) h n")
                             ).then_inc(ctx_in, 16)

            def weights(raw, first, last):
                with sp.Fori(first, last) as c:
                    sp.wait_ge(wffn_in, 16 * c)
                    at_ = c if raw is w_low_raw else c - LOW_CHUNKS
                    sp.dma_start(raw[:, bass.ds(at_, 1), 1, :],
                                 wffn[bass.ds(c, 1)].rearrange("c p n -> p c n")).then_inc(wffn_in, 16)

            sp.wait_ge(w_mm, H * GROUPS)
            sp.wait_ge(xt_lo, B)
            sp.dma_start(w_low_raw[:, 0, 1, :], wffn[0]).then_inc(wffn_in, 16)
            weights(w_low_raw, 1, EARLY_CHUNKS)
            sp.wait_ge(wo_mm, B)
            sp.wait_ge(x2t_mm, GB)
            weights(w_low_raw, EARLY_CHUNKS, LOW_CHUNKS)
            weights(w_high_raw, LOW_CHUNKS, CH)
            with sp.Fori(0, B) as t:
                sp.wait_ge(fin_ok, t + 1)
                sp.dma_start(out[bass.ds(t, 1)].rearrange("b s d -> s b d"),
                             x_sb[:, bass.ds(t, 1), :]).then_inc(stored, 16)
            sp.wait_ge(stored, 16 * B)

        @block.gpsimd
        def _(pool):
            nc.gpsimd.memset(zero_sb[:], 0.0).then_inc(zero_ok, 1)
            nc.gpsimd.memset(ident[:], 0.0).then_inc(id0, 1)
            pool.wait_ge(id0, 1)
            nc.gpsimd.affine_select(out=ident[:], in_=ident[:], compare_op=ALU.not_equal, fill=1.0,
                                    base=0, pattern=[[-1, P]], channel_multiplier=1
                                    ).then_inc(ident_ok, 1)
            for arrived, raw, hi, lo, done in ((wg_in, wg_raw, wg_hi, wg_lo, wg_ok),
                                               (wo_in, wo_raw, wo_hi, wo_lo, wo_ok)):
                pool.wait_ge(arrived, 16)
                nc.gpsimd.tensor_copy(hi[:], raw[:]).then_inc(done, 1)
                pool.wait_ge(done, 1)
                nc.gpsimd.tensor_tensor(lo[:], raw[:], hi[:].bitcast(F32), ALU.subtract
                                        ).then_inc(done, 1)

            def split(raw, parts, first, last):
                with pool.Fori(first, last) as c:
                    i = c - first
                    pool.wait_ge(wffn_in, 16 * (c + 1))
                    loaded = raw[:, bass.ds(i, 1), 1, :]
                    hi, lo = parts[:, bass.ds(i, 1), 0, :], parts[:, bass.ds(i, 1), 1, :]
                    nc.gpsimd.tensor_copy(hi, loaded).then_inc(wffn_hi, 1)
                    pool.drain()
                    nc.gpsimd.tensor_tensor(lo, loaded, hi.bitcast(F32), ALU.subtract
                                            ).then_inc(wffn_ok, 1)

            split(w_low_raw, w_low, 0, LOW_CHUNKS)
            split(w_high_raw, w_high, LOW_CHUNKS, CH)

        @block.tensor
        def _(pe):
            def three(dst, whi, wlo, mhi, mlo, start, stop):
                pe.matmul(dst, whi, mhi, start=start, stop=False)
                pe.matmul(dst, whi, mlo, start=False, stop=False)
                return pe.matmul(dst, wlo, mhi, start=False, stop=stop)

            pe.wait_ge(zero_ok, 1)
            pe.wait_ge(whT_in, 16)
            pe.matmul(bank(S_BANK), zero_sb[:], whT_sb[:].rearrange("p h d -> p (h d)"),
                      start=True, stop=True)
            for h in range(H):
                mm = pe.matmul(bank(T_BANKS[0])[:, h * P:(h + 1) * P], whT_sb[:, h, :], whT_sb[:, h, :],
                               start=True, stop=True)
            mm.then_inc(g_mm, 1)
            pe.wait_ge(g_ok, 1)

            def A_group(g, before_last_w=None):
                pe.wait_ge(ctx_in, 16 * (g + 1))
                for h in range(H):
                    if h >= 2:
                        pe.wait_ge(t_ok, H * g + h - 1)
                    pe.matmul(bank(T_BANKS[h % 2]), g_sb[:, h, :], ctx_sb[:, h, :],
                              start=True, stop=True).then_inc(t_mm, 1)
                for b in range(GB):
                    if b == 0:
                        pe.wait_ge(ident_ok, 1)
                    pe.wait_ge(xn_ok, GB * g + b + 1)
                    if b >= 2:
                        pe.wait_ge(xt_lo, GB * g + b - 1)
                        pe.wait_ge(xt_full, GB * g + b - 1)
                    for k in range(H):
                        mm = pe.transpose(bank(X_BANKS[b % 2])[:, k * P:(k + 1) * P],
                                          z_sb[:, b, k * P:(k + 1) * P], ident[:])
                    mm.then_inc(xt_mm, 1)
                pe.wait_ge(wh_in, 16)
                for b in range(GB):
                    if b < 2:
                        pe.wait_ge(w_ok, H * g)
                    else:
                        pe.wait_ge(v_ok, GB * g + b - 1)
                    for h in range(H):
                        mm = pe.matmul(bank(V_BANKS[b % 2])[:, h * P:(h + 1) * P],
                                       ctx_sb[:, h, b * S:(b + 1) * S], wh_sb[:, h, :],
                                       start=True, stop=True)
                    mm.then_inc(v_mm, 1)
                pe.wait_ge(t_ok, H * (g + 1))
                pe.wait_ge(xt_full, GB * (g + 1))
                for h in range(H):
                    for b in range(GB):
                        mm = pe.matmul(bank(S_BANK)[:, h * P:(h + 1) * P],
                                       t_sb[:, h, b * S:(b + 1) * S], xT_sb[:, h, b, :],
                                       start=False, stop=True, skip_group_check=True)
                mm.then_inc(s_mm, 1)
                pe.wait_ge(xt_lo, GB * (g + 1))
                pe.wait_ge(wg_ok, 2)
                for e in range(H):
                    if e == 2 and before_last_w:
                        before_last_w()
                    if e == 1:
                        pe.wait_ge(v_ok, GB * (g + 1))
                    if e == 3:
                        pe.wait_ge(w_ok, H * g + 1)
                    for k in range(H):
                        cols = slice(e * P, (e + 1) * P)
                        mm = three(bank(W_BANKS[e]), wg_hi[:, k, cols], wg_lo[:, k, cols],
                                   xTh_sb[:, k, :, :].rearrange("p b s -> p (b s)"),
                                   xTl_sb[:, k, :, :].rearrange("p b s -> p (b s)"),
                                   start=(k == 0), stop=(k == H - 1))
                    mm.then_inc(w_mm, 1)

            def O_group(g):
                for h in range(H):
                    mm = pe.matmul(bank(O_BANK0 + h), aT_sb[:, h, :], v_sb[:, h, tiles(g), :],
                                   start=True, stop=True)
                mm.then_inc(o_mm, 1)

            def first_O():
                pe.wait_ge(a_ok, 1)
                pe.wait_ge(t_ok, H * GROUPS)
                pe.wait_ge(xt_lo, B)
                O_group(0)

            def zT_block(g, k):
                if k == 0:
                    pe.wait_ge(z_ok, GB * (g + 1))
                    pe.wait_ge(w_ok, H * GROUPS)
                if k >= 2:
                    pe.wait_ge(wyl_ok, H * g + k - 1)
                for b in range(GB):
                    mm = pe.transpose(bank(Z_BANKS[k % 2])[:, b * S:(b + 1) * S],
                                      z_sb[:, b, k * P:(k + 1) * P], ident[:])
                mm.then_inc(zt_mm, 1)

            def wo_tile(g, b, ahead=None):
                if ahead is not None:
                    pe.wait_ge(x2_ok, ahead)
                for k in range(H):
                    if b == 0:
                        pe.wait_ge(wyl_ok, H * g + k + 1)
                    mm = three(bank(WO_BANKS[b % 2]), wy_hi[:, k, b, :], wy_lo[:, k, b, :],
                               wo_hi[:, k, :], wo_lo[:, k, :], start=(k == 0), stop=(k == H - 1))
                mm.then_inc(wo_mm, 1)

            def x2T_tile(src, dst):
                for k in range(H):
                    mm = pe.transpose(dst[:, k * P:(k + 1) * P], src[:, k * P:(k + 1) * P], ident[:])
                mm.then_inc(x2t_mm, 1)

            A_group(0)
            with pe.Fori(1, GROUPS - 1) as g:
                A_group(g)
            A_group(GROUPS - 1, before_last_w=first_O)
            pe.wait_ge(wo_ok, 2)
            def B_group(g):
                zT_block(g, 0)
                zT_block(g, 1)
                O_group(g + 1)
                zT_block(g, 2)
                zT_block(g, 3)
                for b in range(GB):
                    wo_tile(g, b, GB * g + b - 1 if b >= 2 else GB * g)

            B_group(0)
            with pe.Fori(1, GROUPS - 1) as g:
                B_group(g)
            for k in range(H):
                zT_block(GROUPS - 1, k)
            last = GB * (GROUPS - 1)
            wo_tile(GROUPS - 1, 0, last)
            wo_tile(GROUPS - 1, 1, last)
            for b in range(GB):
                pe.wait_ge(x2n_ok, b + 1)
                x2T_tile(x2n0_sb[:, b, :], bank(O_BANK0 + b))
            wo_tile(GROUPS - 1, 2, last + 1)
            wo_tile(GROUPS - 1, 3, last + 2)

            def gate_up(g, c, first=None):
                n = CH * g + c
                if c == 0:
                    pe.wait_ge(x2l_ok, GB * (g + 1))
                if c >= 2:
                    pe.wait_ge(hdl_ok, n - 1)
                if first:
                    pe.wait_ge(wffn_ok, c + 1)
                    if c == 1:
                        pe.wait_ge(x2_ok, B)
                for j, done in ((0, gate_mm), (1, up_mm)):
                    for k in range(H):
                        cols = slice(j * D + k * P, j * D + (k + 1) * P)
                        mm = three(bank(GU_BANKS[c % 2][j]), chunk_w(c, 0)[:, cols], chunk_w(c, 1)[:, cols],
                                   x2h_sb[:, k, :, :].rearrange("p b s -> p (b s)"),
                                   x2l_sb[:, k, :, :].rearrange("p b s -> p (b s)"),
                                   start=(k == 0), stop=(k == H - 1))
                    mm.then_inc(done, 1)

            def down(g, c):
                if c == 0:
                    pe.wait_ge(fin_ok, GB * g)
                pe.wait_ge(hdl_ok, CH * g + c + 1)
                for b in range(GB):
                    cols = slice(b * S, (b + 1) * S)
                    mm = three(bank(O_BANK0 + b), hd_sb[:, c % 2, 0, cols], hd_sb[:, c % 2, 1, cols],
                               chunk_w(c, 0)[:, 2 * D:], chunk_w(c, 1)[:, 2 * D:],
                               start=(c == 0), stop=(c == CH - 1))
                    if c == CH - 1:
                        mm.then_inc(acc_mm, 1)
                if c < CH - 1:
                    mm.then_inc(down_mm, 1)

            def C_group(g, first=False, last=False):
                for c in range(CH):
                    gate_up(g, c, first)
                    if c:
                        if c < CH - 1:
                            down(g, c - 1)
                if not last:
                    for b in (0, 1):
                        if b == 0:
                            pe.wait_ge(hdl_ok, CH * g + CH - 1)
                        pe.wait_ge(x2n_ok, GB * (g + 1) + b + 1)
                        x2T_tile(x2n_sb[:, b, :], bank(GU_BANKS[1][b]))
                down(g, CH - 2)
                if not last:
                    for b in (2, 3):
                        if b == 2:
                            pe.wait_ge(hdl_ok, CH * g + CH)
                        pe.wait_ge(x2n_ok, GB * (g + 1) + b + 1)
                        x2T_tile(x2n_sb[:, b, :], bank(GU_BANKS[0][b - 2]))
                down(g, CH - 1)

            C_group(0, first=True)
            with pe.Fori(1, GROUPS - 1) as g:
                C_group(g)
            C_group(GROUPS - 1, last=True)

        @block.scalar
        def _(act):
            act.wait_ge(small_in, 32)
            nc.scalar.activation(tg[:], small[:, TG0:TG0 + 2], ACT.Tanh).then_inc(tanh_ok, 1)
            act.wait_ge(eps_ok, 2)
            act.wait_ge(g_mm, 1)
            nc.scalar.activation(g_sb[:].rearrange("p h d -> p (h d)"), bank(T_BANKS[0]), ACT.Copy
                                 ).then_inc(g_ok, 1)

            def A_group(g):
                act.wait_ge(mv_ok, GB * (g + 1))
                act.wait_ge(rstd_ok, g)
                nc.scalar.activation(std[:], mv[:, :, 1], ACT.Sqrt, bias=eps[:, 0:1]).then_inc(std_ok, 1)
                act.wait_ge(s_mm, g)
                for h in range(H):
                    act.wait_ge(t_mm, H * g + h + 1)
                    nc.scalar.activation(t_sb[:, h, :], bank(T_BANKS[h % 2]), ACT.Copy).then_inc(t_ok, 1)
                act.wait_ge(w_mm, H * g)
                for b in range(GB):
                    act.wait_ge(xt_mm, GB * g + b + 1)
                    src = bank(X_BANKS[b % 2]).rearrange("p (k s) -> p k s", k=H)
                    nc.scalar.activation(xT_sb[:, :, b, :], src, ACT.Copy).then_inc(xt_full, 1)
                    nc.scalar.activation(xTh_sb[:, :, b, :], src, ACT.Copy).then_inc(xt_hi, 1)
                for b in range(GB):
                    act.wait_ge(v_mm, GB * g + b + 1)
                    src = bank(V_BANKS[b % 2]).rearrange("p (h e) -> p h e", h=H)
                    nc.scalar.activation(v_sb[:, :, g * GB + b, :], src, ACT.Copy).then_inc(v_ok, 1)
                for e in range(H):
                    act.wait_ge(w_mm, H * g + e + 1)
                    nc.scalar.activation(wT_sb[:, e, tokens(g)], bank(W_BANKS[e]), ACT.Relu
                                         ).then_inc(w_ok, 1)

            A_group(0)
            with act.Fori(1, GROUPS) as g:
                A_group(g)

            def std_tile(g, b):
                act.wait_ge(mv_ok, B + GB * g + b + 1)
                nc.scalar.activation(std[:, b:b + 1], mv[:, b, 1:2], ACT.Sqrt, bias=eps[:, 1:2]
                                     ).then_inc(std_ok, 1)

            def y_block(g, k):
                act.wait_ge(zt_mm, H * g + k + 1)
                nc.scalar.activation(bank(Z_BANKS[k % 2]), bank(Z_BANKS[k % 2]), ACT.Identity,
                                     scale=small[:, GAM0 + k:GAM0 + k + 1],
                                     bias=small[:, BET0 + k:BET0 + k + 1]).then_inc(y_ok, 1)

            def wy_hi_block(g, k):
                act.wait_ge(wy_ok, H * g + k + 1)
                if k == 0:
                    act.wait_ge(wo_mm, GB * g)
                nc.scalar.activation(wy_hi[:, k, :, :].rearrange("p b s -> p (b s)"),
                                     bank(Z_BANKS[k % 2]), ACT.Copy).then_inc(wyh_ok, 1)

            def wy_blocks(g):
                for k in (0, 2):
                    y_block(g, k)
                    y_block(g, k + 1)
                    wy_hi_block(g, k)
                    wy_hi_block(g, k + 1)

            def std2_group(g):
                act.wait_ge(mv2_ok, GB * (g + 1))
                nc.scalar.activation(std2[:, tiles(g)], l_mv[:, :, 1], ACT.Sqrt, bias=eps[:, 0:1]
                                     ).then_inc(std2_ok, 1)

            def x2_hi(g, b, src):
                act.wait_ge(x2t_mm, GB * g + b + 1)
                nc.scalar.activation(x2h_sb[:, :, b, :], src.rearrange("p (k s) -> p k s", k=H), ACT.Copy
                                     ).then_inc(x2h_ok, 1)

            for b in range(GB):
                std_tile(0, b)
            def B_group(g):
                wy_blocks(g)
                for b in range(GB):
                    std_tile(g + 1, b)
                std2_group(g)

            B_group(0)
            with act.Fori(1, GROUPS - 1) as g:
                B_group(g)
            wy_blocks(GROUPS - 1)
            for b in range(GB):
                x2_hi(0, b, bank(O_BANK0 + b))
            std2_group(GROUPS - 1)

            def C_group(g, last=False):
                for c in range(CH):
                    n = CH * g + c
                    act.wait_ge(gate_mm, n + 1)
                    if c >= 2:
                        act.wait_ge(hd_ok, n - 1)
                    nc.scalar.activation(silu_sb[:, c % 2, :], bank(GU_BANKS[c % 2][0]), ACT.Silu,
                                         scale=small[:, GS0 + c:GS0 + c + 1]).then_inc(silu_ok, 1)
                    act.wait_ge(hd_ok, n + 1)
                    if c >= 2:
                        act.wait_ge(down_mm, (CH - 1) * g + c - 1)
                    elif c == 0:
                        act.wait_ge(acc_mm, GB * g)
                    nc.scalar.activation(hd_sb[:, c % 2, 0, :], bank(GU_BANKS[c % 2][1]), ACT.Copy
                                         ).then_inc(hdh_ok, 1)
                if not last:
                    for b in range(GB):
                        x2_hi(g + 1, b, bank(GU_BANKS[1 - b // 2][b % 2]))

            C_group(0)
            with act.Fori(1, GROUPS - 1) as g:
                C_group(g)
            C_group(GROUPS - 1, last=True)

        @block.vector
        def _(dve):
            nc.vector.memset(eps[:, 0:1], LN_EPS).then_inc(eps_ok, 1)
            nc.vector.memset(eps[:, 1:2], GN_EPS).then_inc(eps_ok, 1)
            dve.wait_ge(tanh_ok, 1)
            nc.vector.tensor_scalar(dsg_sb[:], dsg_sb[:], tg[:, 1:2], None, ALU.mult).then_inc(dsg_ok, 1)

            def standing():
                nc.vector.memset(carrier[:], 0.0)

            def A_group(g):
                dve.wait_ge(x_in, 16 * (g + 1))
                standing()
                dve.wait_ge(mv_ok, GB * g)
                for b in range(GB):
                    nc.vector.bn_stats(st6[:, b, :], x_sb[:, g * GB + b, :]).then_inc(st_ok, 1)
                dve.drain()
                for b in range(GB):
                    nc.vector.bn_aggr(mv[:, b, :], st6[:, b, :]).then_inc(mv_ok, 1)
                dve.wait_ge(std_ok, g + 1)
                nc.vector.reciprocal(rstd[:], std[:]).then_inc(rstd_ok, 1)
                dve.wait_ge(rstd_ok, g + 1)
                dve.wait_ge(mv_ok, GB * (g + 1))
                dve.wait_ge(xt_mm, GB * g)
                for b in range(GB):
                    nc.vector.tensor_scalar(z_sb[:, b, :], x_sb[:, g * GB + b, :], mv[:, b, 0:1],
                                            rstd[:, b:b + 1], ALU.subtract, ALU.mult).then_inc(xn_ok, 1)
                for b in range(GB):
                    dve.wait_ge(xt_hi, GB * g + b + 1)
                    nc.vector.tensor_tensor(
                        xTl_sb[:, :, b, :], bank(X_BANKS[b % 2]).rearrange("p (k s) -> p k s", k=H),
                        xTh_sb[:, :, b, :].bitcast(F32), ALU.subtract).then_inc(xt_lo, 1)

            A_group(0)
            with dve.Fori(1, GROUPS) as g:
                A_group(g)

            dve.wait_ge(s_mm, GROUPS)
            dve.wait_ge(mask_in, 16)
            nc.vector.tensor_tensor(aT_sb[:].rearrange("p h s -> p (h s)"), bank(S_BANK),
                                    mask_sb[:].rearrange("p h s -> p (h s)"), ALU.mult).then_inc(am_ok, 1)
            dve.wait_ge(am_ok, 1)
            flat = aT_sb[:].rearrange("p h s -> p (h s)")
            nc.vector.scalar_tensor_tensor(flat, flat, -1.0, flat, ALU.mult, ALU.max).then_inc(am_ok, 1)
            dve.wait_ge(am_ok, 2)
            nc.vector.tensor_scalar(flat, flat, 1.0, None, ALU.max).then_inc(a_ok, 1)

            def O_stats(g, b):
                if b == 0:
                    dve.wait_ge(o_mm, g + 1)
                n = B + GB * g + b
                nc.vector.bn_stats(st6[:, b, :], ps[:, O_BANK0:O_BANK0 + H, b * P:(b + 1) * P]
                                   ).then_inc(st_ok, 1)
                dve.drain()
                nc.vector.bn_aggr(mv[:, b, :], st6[:, b, :]).then_inc(mv_ok, 1)

            def O_norm(g, b):
                dve.wait_ge(std_ok, GROUPS + GB * g + b + 1)
                nc.vector.reciprocal(rstd[:, b:b + 1], std[:, b:b + 1]).then_inc(rstd_ok, 1)
                dve.wait_ge(rstd_ok, GROUPS + GB * g + b + 1)
                if b == 0:
                    dve.wait_ge(zt_mm, H * g)
                nc.vector.tensor_scalar(z_sb[:, b, :].rearrange("p (h e) -> p h e", h=H),
                                        ps[:, O_BANK0:O_BANK0 + H, b * P:(b + 1) * P],
                                        mv[:, b, 0:1], rstd[:, b:b + 1], ALU.subtract, ALU.mult
                                        ).then_inc(z_ok, 1)

            def wy_blocks(g):
                for k0 in (0, 2):
                    for k in (k0, k0 + 1):
                        dve.wait_ge(y_ok, H * g + k + 1)
                        nc.vector.tensor_tensor(bank(Z_BANKS[k % 2]), bank(Z_BANKS[k % 2]),
                                                wT_sb[:, k, tokens(g)], ALU.mult).then_inc(wy_ok, 1)
                    for k in (k0, k0 + 1):
                        dve.wait_ge(wyh_ok, H * g + k + 1)
                        nc.vector.tensor_tensor(wy_lo[:, k, :, :].rearrange("p b s -> p (b s)"),
                                                bank(Z_BANKS[k % 2]),
                                                wy_hi[:, k, :, :].rearrange("p b s -> p (b s)").bitcast(F32),
                                                ALU.subtract).then_inc(wyl_ok, 1)

            def residual(g, b):
                t = g * GB + b
                dve.wait_ge(wo_mm, t + 1)
                nc.vector.scalar_tensor_tensor(x_sb[:, t, :], bank(WO_BANKS[b % 2]), tg[:, 0:1],
                                               x_sb[:, t, :], ALU.mult, ALU.add).then_inc(x2_ok, 1)

            def x2_stats(g, b):
                t = g * GB + b
                dve.wait_ge(x2_ok, t + 1)
                standing()
                nc.vector.bn_stats(l_st6[:, b, :], x_sb[:, t, :]).then_inc(lst_ok, 1)
                dve.drain()
                nc.vector.bn_aggr(l_mv[:, b, :], l_st6[:, b, :]).then_inc(mv2_ok, 1)

            def x2_rstd(g):
                dve.wait_ge(mv2_ok, GB * (g + 1))
                nc.vector.tensor_copy(mean2[:, tiles(g)], l_mv[:, :, 0]).then_inc(mean2_ok, 1)
                dve.wait_ge(std2_ok, g + 1)
                nc.vector.reciprocal(rstd2[:, tiles(g)], std2[:, tiles(g)]).then_inc(rstd2_ok, 1)

            def x2_norm(dst, g, b):
                t = g * GB + b
                nc.vector.tensor_scalar(dst[:, b, :], x_sb[:, t, :], mean2[:, bass.ds(t, 1)], rstd2[:, bass.ds(t, 1)],
                                        ALU.subtract, ALU.mult).then_inc(x2n_ok, 1)

            def x2_lo(g, b, src):
                dve.wait_ge(x2h_ok, GB * g + b + 1)
                nc.vector.tensor_tensor(x2l_sb[:, :, b, :], src.rearrange("p (k s) -> p k s", k=H),
                                        x2h_sb[:, :, b, :].bitcast(F32), ALU.subtract).then_inc(x2l_ok, 1)

            for b in range(GB):
                O_stats(0, b)
            for b in range(GB):
                O_norm(0, b)
            def B_group(g):
                wy_blocks(g)
                for b in range(GB):
                    O_stats(g + 1, b)
                    residual(g, b)
                    O_norm(g + 1, b)
                    x2_stats(g, b)
                x2_rstd(g)

            B_group(0)
            with dve.Fori(1, GROUPS - 1) as g:
                B_group(g)
            wy_blocks(GROUPS - 1)
            dve.wait_ge(rstd2_ok, 1)
            dve.wait_ge(mean2_ok, 1)
            for b in range(GB):
                x2_norm(x2n0_sb, 0, b)
            for b in range(2):
                residual(GROUPS - 1, b)
                x2_stats(GROUPS - 1, b)
            for b in range(GB):
                x2_lo(0, b, bank(O_BANK0 + b))
            for b in range(2, GB):
                residual(GROUPS - 1, b)
                x2_stats(GROUPS - 1, b)
            x2_rstd(GROUPS - 1)

            def C_group(g, last=False):
                for c in range(CH):
                    n = CH * g + c
                    dve.wait_ge(silu_ok, n + 1)
                    dve.wait_ge(up_mm, n + 1)
                    u = bank(GU_BANKS[c % 2][1])
                    nc.vector.scalar_tensor_tensor(u, u, small[:, US0 + c:US0 + c + 1], silu_sb[:, c % 2, :],
                                                   ALU.mult, ALU.mult).then_inc(hd_ok, 1)
                    dve.wait_ge(hdh_ok, n + 1)
                    nc.vector.tensor_tensor(hd_sb[:, c % 2, 1, :], u, hd_sb[:, c % 2, 0, :].bitcast(F32),
                                            ALU.subtract).then_inc(hdl_ok, 1)
                    if not last and 3 <= c < 3 + GB:
                        if c == 3:
                            dve.wait_ge(x2t_mm, GB * (g + 1))
                            dve.wait_ge(rstd2_ok, g + 2)
                            dve.wait_ge(mean2_ok, g + 2)
                        x2_norm(x2n_sb, g + 1, c - 3)
                if not last:
                    for b in range(GB):
                        x2_lo(g + 1, b, bank(GU_BANKS[1 - b // 2][b % 2]))
                for b in range(GB):
                    t = g * GB + b
                    dve.wait_ge(acc_mm, t + 1)
                    acc = bank(O_BANK0 + b)
                    nc.vector.tensor_tensor(acc, acc, dsg_sb[:], ALU.mult).then_inc(sc_ok, 1)
                    dve.wait_ge(sc_ok, t + 1)
                    nc.vector.tensor_tensor(x_sb[:, t, :], acc, x_sb[:, t, :], ALU.add).then_inc(fin_ok, 1)

            C_group(0)
            with dve.Fori(1, GROUPS - 1) as g:
                C_group(g)
            C_group(GROUPS - 1, last=True)


def decay_mask():
    gam = (1.0 - 2.0 ** (-5.0 - np.arange(H, dtype=np.float32))).astype(np.float32)
    idx = np.arange(S, dtype=np.float32)
    expo = idx[None, :] - idx[:, None]
    d = np.where(expo[None] <= 0, gam[:, None, None] ** expo[None], np.float32(0))
    d = d / np.sqrt(d.sum(axis=-1))[:, None, :] / np.sqrt(np.float32(P))
    return np.ascontiguousarray(d.transpose(2, 0, 1).astype(np.float32))


def kernel(**inputs):
    import concourse.bacc as bacc
    from concourse.bass_utils import run_bass_kernel_spmd

    a = {n: np.asarray(v) for n, v in inputs.items()}

    def rows(w):
        return w.reshape(-1, P, w.shape[-1]).transpose(1, 0, 2)

    def up_cols(w):
        return w.reshape(CH, P, H, P).transpose(0, 3, 2, 1).reshape(CH, P, D)

    Wh = a["L0_xattn_Wh"]
    data = {
        "x": a["x"],
        "ctxT": a["ctx_2048"].reshape(GROUPS, GB, S, H, P).transpose(0, 4, 3, 1, 2).reshape(GROUPS, P, H, NT),
        "WhT": Wh.transpose(2, 0, 1),
        "Wh": Wh.transpose(1, 0, 2),
        "wg": rows(a["L0_xattn_wg_w"]),
        "wo": rows(a["L0_xattn_wo_w"]),
        "wffn": np.concatenate([up_cols(a["L0_ffn_gate_w"]), up_cols(a["L0_ffn_up_w"]),
                                a["L0_ffn_down_w"].T.reshape(CH, P, D)], axis=2),
        "smalls": np.concatenate(
            [a["L0_ffn_gate_s"].reshape(CH, P).T, a["L0_ffn_up_s"].reshape(CH, P).T,
             a["L0_xattn_gn_gamma"].reshape(H, P).T, a["L0_xattn_gn_beta"].reshape(H, P).T,
             np.broadcast_to(a["g_xattn"].reshape(1, 1), (P, 1)),
             np.broadcast_to(a["g_ffn"].reshape(1, 1), (P, 1))], axis=1),
        "down_s": a["L0_ffn_down_s"].reshape(1, D),
        "mask": decay_mask(),
    }
    nc = bacc.Bacc("TRN2", target_bir_lowering=False, num_devices=1)
    arrays, args = {}, []
    for name, v in data.items():
        v = np.ascontiguousarray(v)
        arrays[f"in_{name}"] = v
        args.append(nc.dram_tensor(f"in_{name}", v.shape, mybir.dt.from_np(v.dtype), kind="ExternalInput").ap())
    args.append(nc.dram_tensor("out_x", (B, S, D), F32, kind="ExternalOutput").ap())
    build(nc, *args)
    r = run_bass_kernel_spmd(nc, [arrays], core_ids=[0])
    return r.results[0]["out_x"]
```

```python
from contextlib import ExitStack

import numpy as np

import concourse.bass as bass
from concourse import mybir

F32 = mybir.dt.float32
F32R = mybir.dt.float32r
ALU = mybir.AluOpType
ACT = mybir.ActivationFunctionType
AX_X = mybir.AxisListType.X

P = 128
B, S, D = 16, 128, 512
H = D // P
INTER = 1408
CH = INTER // P
GB = 4
GROUPS = B // GB
NT = GB * S
LN_EPS = 1e-5
GN_EPS = 1e-3

S_BANK = 0
T_BANKS = (1, 2)
X_BANKS = (3, 4, 1, 2)
V_BANKS = (5, 6)
W_BANKS = (7, 5, 6, 7)
O_BANK0 = 1
Z_BANKS = (5, 6)
WO_BANKS = (7, 0)
GU_BANKS = ((5, 6), (7, 0))

GS0, US0, GAM0, BET0, TG0 = 0, CH, 2 * CH, 2 * CH + H, 2 * CH + 2 * H
N_SMALL = TG0 + 2
WROW = 3 * D
LOW_CHUNKS = 6
EARLY_CHUNKS = 4

KB = 1024


def build(nc, x, ctxT, WhT, Wh, wg, wo, wffn, smalls, down_s, mask, out):
    base = -(-nc.sbuf_base // 64) * 64
    with ExitStack() as ctx:
        def at(name, offset, shape, dt=F32):
            return nc.alloc_sbuf_tensor_at(name, [P] + shape, dt, offset=base + int(offset))

        def sem(name):
            return ctx.enter_context(nc.semaphore(name))

        x_sb = at("x_sb", 0, [B, D])
        v_sb = at("v_sb", 32 * KB, [H, B, P])
        wT_sb = at("wT_sb", 64 * KB, [H, B * S])
        ctx_sb = at("ctx_sb", 96 * KB, [H, NT])
        t_sb = at("t_sb", 112 * KB, [H, NT])
        xT_sb = at("xT_sb", 120 * KB, [H, GB, S])
        xTh_sb = at("xTh_sb", 128 * KB, [H, GB, S], F32R)
        xTl_sb = at("xTl_sb", 136 * KB, [H, GB, S], F32R)
        wg_hi = at("wg_hi", 144 * KB, [H, D], F32R)
        wg_raw = at("wg_raw", 152 * KB, [H, D])
        wg_lo = at("wg_lo", 152 * KB, [H, D], F32R)
        wh_sb = at("wh_sb", 160 * KB, [H, P])
        whT_sb = at("whT_sb", 162 * KB, [H, P])
        g_sb = at("g_sb", 164 * KB, [H, P])
        mask_sb = at("mask_sb", 166 * KB, [H, P])
        wy_hi = at("wy_hi", 144 * KB, [H, GB, S], F32R)
        wy_lo = at("wy_lo", 152 * KB, [H, GB, S], F32R)
        x2n0_sb = at("x2n0_sb", 160 * KB, [GB, D])
        w_low = at("w_low", 96 * KB, [LOW_CHUNKS, 2, WROW], F32R)
        w_low_raw = at("w_low_raw", 96 * KB, [LOW_CHUNKS, 2, WROW])
        w_high = at("w_high", 32 * KB, [CH - LOW_CHUNKS, 2, WROW], F32R)
        w_high_raw = at("w_high_raw", 32 * KB, [CH - LOW_CHUNKS, 2, WROW])
        silu_sb = at("silu_sb", 92 * KB, [2, NT])
        wo_hi = at("wo_hi", 168 * KB, [H, D], F32R)
        wo_raw = at("wo_raw", 176 * KB, [H, D])
        wo_lo = at("wo_lo", 176 * KB, [H, D], F32R)
        hd_sb = at("hd_sb", 168 * KB, [2, 2, NT], F32R)
        x2n_sb = at("x2n_sb", 176 * KB, [GB, D])
        z_sb = at("z_sb", 184 * KB, [GB, D])
        x2h_sb = at("x2h_sb", 184 * KB, [H, GB, S], F32R)
        x2l_sb = at("x2l_sb", 192 * KB, [H, GB, S], F32R)
        top = 200 * KB
        aT_sb = at("aT_sb", top, [H, P])
        dsg_sb = at("dsg_sb", top + 2 * KB, [D])
        ident = at("ident", top + 4 * KB, [P])
        zero_sb = at("zero_sb", top + 4.5 * KB, [P])
        small = at("small", top + 5 * KB, [N_SMALL])
        tg = at("tg", top + 5.25 * KB, [2])
        eps = at("eps", top + 5.3125 * KB, [2])
        st6 = at("st6", top + 5.375 * KB, [GB, 6])
        mv = at("mv", top + 5.5 * KB, [GB, 2])
        std = at("std", top + 5.5625 * KB, [GB])
        rstd = at("rstd", top + 5.625 * KB, [GB])
        l_st6 = at("l_st6", top + 5.75 * KB, [B, 6])
        l_mv = at("l_mv", top + 6.125 * KB, [B, 2])
        std2 = at("std2", top + 6.25 * KB, [B])
        lomax = at("lomax", top + 6.5 * KB, [CH + 1])
        loall = at("loall", top + 6.5625 * KB, [1])
        flag = at("flag", top + 6.59375 * KB, [1], mybir.dt.int32)
        carrier = at("carrier", top + 6.375 * KB, [1])
        rstd2 = at("rstd2", top + 6.3125 * KB, [B])

        ps = ctx.enter_context(nc.psum_tensor("ps", [P, 8, 512], F32))

        whT_in, wh_in, small_in, mask_in = sem("whT_in"), sem("wh_in"), sem("small_in"), sem("mask_in")
        wg_in, wo_in, ds_in = sem("wg_in"), sem("wo_in"), sem("ds_in")
        x_in, ctx_in = sem("x_in"), sem("ctx_in")
        wffn_in = sem("wffn_in")
        ident_ok, zero_ok, eps_ok = sem("ident_ok"), sem("zero_ok"), sem("eps_ok")
        id0 = sem("id0")
        wg_ok, wo_ok = sem("wg_ok"), sem("wo_ok")
        wffn_hi, wffn_ok = sem("wffn_hi"), sem("wffn_ok")
        tanh_ok, dsg_ok = sem("tanh_ok"), sem("dsg_ok")
        g_mm, g_ok = sem("g_mm"), sem("g_ok")
        st_ok, mv_ok = sem("st_ok"), sem("mv_ok")
        std_ok, rstd_ok = sem("std_ok"), sem("rstd_ok")
        xn_ok, xt_mm = sem("xn_ok"), sem("xt_mm")
        xt_full, xt_hi, xt_lo = sem("xt_full"), sem("xt_hi"), sem("xt_lo")
        t_mm, t_ok = sem("t_mm"), sem("t_ok")
        v_mm, v_ok = sem("v_mm"), sem("v_ok")
        s_mm = sem("s_mm")
        w_mm, w_ok = sem("w_mm"), sem("w_ok")
        am_ok, a_ok = sem("am_ok"), sem("a_ok")
        o_mm, z_ok = sem("o_mm"), sem("z_ok")
        zt_mm, y_ok, wy_ok, wyh_ok, wyl_ok = (
            sem("zt_mm"), sem("y_ok"), sem("wy_ok"), sem("wyh_ok"), sem("wyl_ok"))
        wo_mm, x2_ok = sem("wo_mm"), sem("x2_ok")
        lst_ok, mv2_ok = sem("lst_ok"), sem("mv2_ok")
        std2_ok, rstd2_ok = sem("std2_ok"), sem("rstd2_ok")
        x2n_ok, x2t_mm, x2h_ok, x2l_ok = (
            sem("x2n_ok"), sem("x2t_mm"), sem("x2h_ok"), sem("x2l_ok"))
        gate_mm, up_mm, silu_ok = sem("gate_mm"), sem("up_mm"), sem("silu_ok")
        hd_ok, hdh_ok, hdl_ok, down_mm = sem("hd_ok"), sem("hdh_ok"), sem("hdl_ok"), sem("down_mm")
        acc_mm, sc_ok, fin_ok = sem("acc_mm"), sem("sc_ok"), sem("fin_ok")
        stored = sem("stored")
        lomax_ok, loany_ok, loall_ok, flag_ok = sem("lomax_ok"), sem("loany_ok"), sem("loall_ok"), sem("flag_ok")

        def bank(i):
            return ps[:, i, :]

        def tiles(g):
            return bass.ds(g * GB, GB)

        def tokens(g):
            return bass.ds(g * NT, NT)

        def chunk_w(c, part):
            return w_low[:, c, part, :] if c < LOW_CHUNKS else w_high[:, c - LOW_CHUNKS, part, :]

        block = ctx.enter_context(nc.Block())

        @block.sync
        def _(sp):
            sp.dma_start(small[:], smalls).then_inc(small_in, 16)
            sp.dma_start(whT_sb[:], WhT).then_inc(whT_in, 16)
            sp.dma_start(x_sb[:, 0:GB, :], x[0:GB].rearrange("b s d -> s b d")).then_inc(x_in, 16)
            sp.dma_start(ctx_sb[:], ctxT[0]).then_inc(ctx_in, 16)
            sp.dma_start(wh_sb[:], Wh).then_inc(wh_in, 16)
            sp.dma_start(wg_raw[:], wg).then_inc(wg_in, 16)
            sp.dma_start(wo_raw[:], wo).then_inc(wo_in, 16)
            sp.dma_start(mask_sb[:], mask).then_inc(mask_in, 16)
            sp.dma_start(dsg_sb[:], down_s.to_broadcast([P, D])).then_inc(ds_in, 16)
            with sp.Fori(1, GROUPS) as g:
                sp.wait_ge(x_in, 16 * g)
                sp.dma_start(x_sb[:, tiles(g), :],
                             x[tiles(g)].rearrange("b s d -> s b d")).then_inc(x_in, 16)
                sp.wait_ge(ctx_in, 16 * g)
                sp.wait_ge(v_mm, GB * g)
                sp.dma_start(ctx_sb[:], ctxT[bass.ds(g, 1)].rearrange("g p h n -> (g p) h n")
                             ).then_inc(ctx_in, 16)

            def weights(raw, first, last):
                with sp.Fori(first, last) as c:
                    sp.wait_ge(wffn_in, 16 * c)
                    at_ = c if raw is w_low_raw else c - LOW_CHUNKS
                    sp.dma_start(raw[:, bass.ds(at_, 1), 1, :],
                                 wffn[bass.ds(c, 1)].rearrange("c p n -> p c n")).then_inc(wffn_in, 16)

            sp.wait_ge(w_mm, H * GROUPS)
            sp.wait_ge(xt_lo, B)
            sp.dma_start(w_low_raw[:, 0, 1, :], wffn[0]).then_inc(wffn_in, 16)
            weights(w_low_raw, 1, EARLY_CHUNKS)
            sp.wait_ge(wo_mm, B)
            sp.wait_ge(x2t_mm, GB)
            weights(w_low_raw, EARLY_CHUNKS, LOW_CHUNKS)
            weights(w_high_raw, LOW_CHUNKS, CH)
            with sp.Fori(0, B) as t:
                sp.wait_ge(fin_ok, t + 1)
                sp.dma_start(out[bass.ds(t, 1)].rearrange("b s d -> s b d"),
                             x_sb[:, bass.ds(t, 1), :]).then_inc(stored, 16)
            sp.wait_ge(stored, 16 * B)

        @block.gpsimd
        def _(pool):
            nc.gpsimd.memset(zero_sb[:], 0.0).then_inc(zero_ok, 1)
            nc.gpsimd.memset(ident[:], 0.0).then_inc(id0, 1)
            pool.wait_ge(id0, 1)
            nc.gpsimd.affine_select(out=ident[:], in_=ident[:], compare_op=ALU.not_equal, fill=1.0,
                                    base=0, pattern=[[-1, P]], channel_multiplier=1
                                    ).then_inc(ident_ok, 1)
            for arrived, raw, hi, lo, done in ((wg_in, wg_raw, wg_hi, wg_lo, wg_ok),
                                               (wo_in, wo_raw, wo_hi, wo_lo, wo_ok)):
                pool.wait_ge(arrived, 16)
                nc.gpsimd.tensor_copy(hi[:], raw[:]).then_inc(done, 1)
                pool.wait_ge(done, 1)
                nc.gpsimd.tensor_tensor(lo[:], raw[:], hi[:].bitcast(F32), ALU.subtract
                                        ).then_inc(done, 1)

            def split(raw, parts, first, last):
                with pool.Fori(first, last) as c:
                    i = c - first
                    pool.wait_ge(wffn_in, 16 * (c + 1))
                    loaded = raw[:, bass.ds(i, 1), 1, :]
                    hi, lo = parts[:, bass.ds(i, 1), 0, :], parts[:, bass.ds(i, 1), 1, :]
                    nc.gpsimd.tensor_copy(hi, loaded).then_inc(wffn_hi, 1)
                    pool.drain()
                    nc.gpsimd.tensor_tensor(lo, loaded, hi.bitcast(F32), ALU.subtract
                                            ).then_inc(wffn_ok, 1)

            split(w_low_raw, w_low, 0, LOW_CHUNKS)
            split(w_high_raw, w_high, LOW_CHUNKS, CH)
            pool.wait_ge(loany_ok, 1)
            nc.gpsimd.partition_all_reduce(loall[:], lomax[:, CH:], P, bass.bass_isa.ReduceOp.max
                                           ).then_inc(loall_ok, 1)

        @block.tensor
        def _(pe):
            def three(dst, whi, wlo, mhi, mlo, start, stop):
                pe.matmul(dst, whi, mhi, start=start, stop=False)
                pe.matmul(dst, whi, mlo, start=False, stop=False)
                return pe.matmul(dst, wlo, mhi, start=False, stop=stop)

            pe.wait_ge(zero_ok, 1)
            pe.wait_ge(whT_in, 16)
            pe.matmul(bank(S_BANK), zero_sb[:], whT_sb[:].rearrange("p h d -> p (h d)"),
                      start=True, stop=True)
            for h in range(H):
                mm = pe.matmul(bank(T_BANKS[0])[:, h * P:(h + 1) * P], whT_sb[:, h, :], whT_sb[:, h, :],
                               start=True, stop=True)
            mm.then_inc(g_mm, 1)
            pe.wait_ge(g_ok, 1)
            pe.wait_ge(ident_ok, 1)

            def A_group(g, before_last_w=None):
                pe.wait_ge(ctx_in, 16 * (g + 1))
                pe.wait_ge(xt_lo, GB * g)
                for h in range(H):
                    if h >= 2:
                        pe.wait_ge(t_ok, H * g + h - 1)
                    pe.matmul(bank(T_BANKS[h % 2]), g_sb[:, h, :], ctx_sb[:, h, :],
                              start=True, stop=True).then_inc(t_mm, 1)
                pe.wait_ge(wh_in, 16)
                pe.wait_ge(w_ok, H * g)
                for b0 in (0, 2):
                    for b in (b0, b0 + 1):
                        if b >= 2:
                            pe.wait_ge(v_ok, GB * g + b - 1)
                        for h in range(H):
                            mm = pe.matmul(bank(V_BANKS[b % 2])[:, h * P:(h + 1) * P],
                                           ctx_sb[:, h, b * S:(b + 1) * S], wh_sb[:, h, :],
                                           start=True, stop=True)
                        mm.then_inc(v_mm, 1)
                    for b in (b0, b0 + 1):
                        pe.wait_ge(xn_ok, GB * g + b + 1)
                        if b == 2:
                            pe.wait_ge(t_ok, H * (g + 1))
                        for k in range(H):
                            mm = pe.transpose(bank(X_BANKS[b])[:, k * P:(k + 1) * P],
                                              z_sb[:, b, k * P:(k + 1) * P], ident[:])
                        mm.then_inc(xt_mm, 1)
                pe.wait_ge(t_ok, H * (g + 1))
                for b in range(GB):
                    pe.wait_ge(xt_full, GB * g + b + 1)
                    for h in range(H):
                        mm = pe.matmul(bank(S_BANK)[:, h * P:(h + 1) * P],
                                       t_sb[:, h, b * S:(b + 1) * S], xT_sb[:, h, b, :],
                                       start=False, stop=True, skip_group_check=True)
                mm.then_inc(s_mm, 1)
                pe.wait_ge(xt_lo, GB * (g + 1))
                pe.wait_ge(wg_ok, 2)
                for e in range(H):
                    if e == 1 and before_last_w:
                        before_last_w()
                    if e == 1:
                        pe.wait_ge(v_ok, GB * (g + 1))
                    if e == 3:
                        pe.wait_ge(w_ok, H * g + 1)
                    for k in range(H):
                        cols = slice(e * P, (e + 1) * P)
                        mm = three(bank(W_BANKS[e]), wg_hi[:, k, cols], wg_lo[:, k, cols],
                                   xTh_sb[:, k, :, :].rearrange("p b s -> p (b s)"),
                                   xTl_sb[:, k, :, :].rearrange("p b s -> p (b s)"),
                                   start=(k == 0), stop=(k == H - 1))
                    mm.then_inc(w_mm, 1)

            def O_heads(g, heads):
                for h in heads:
                    mm = pe.matmul(bank(O_BANK0 + h), aT_sb[:, h, :], v_sb[:, h, tiles(g), :],
                                   start=True, stop=True)
                if h == H - 1:
                    mm.then_inc(o_mm, 1)

            def first_O():
                pe.wait_ge(a_ok, 1)
                pe.wait_ge(t_ok, H * GROUPS)
                pe.wait_ge(xt_lo, B)
                O_heads(0, range(H))

            def ahead_of_first(g):
                return not (isinstance(g, int) and g == 0)

            def zT_block(g, k):
                if k == 0:
                    pe.wait_ge(z_ok, GB * (g + 1))
                    pe.wait_ge(w_ok, H * GROUPS)
                if k >= 2:
                    pe.wait_ge(wyl_ok, H * g + k - 1)
                elif ahead_of_first(g):
                    pe.wait_ge(wyl_ok, H * g + k - 1)
                for b in range(GB):
                    mm = pe.transpose(bank(Z_BANKS[k % 2])[:, b * S:(b + 1) * S],
                                      z_sb[:, b, k * P:(k + 1) * P], ident[:])
                mm.then_inc(zt_mm, 1)

            def wo_part(g, b, k):
                pe.wait_ge(wyl_ok, H * g + k + 1)
                return three(bank(WO_BANKS[b % 2]), wy_hi[:, k, b, :], wy_lo[:, k, b, :],
                             wo_hi[:, k, :], wo_lo[:, k, :], start=(k == 0), stop=(k == H - 1))

            def wo_first_tiles(g):
                pe.wait_ge(x2_ok, GB * g)
                for k0 in (0, 2):
                    for b in (0, 1):
                        for k in (k0, k0 + 1):
                            mm = wo_part(g, b, k)
                        if k0 == 2:
                            mm.then_inc(wo_mm, 1)

            def wo_tile(g, b):
                pe.wait_ge(x2_ok, GB * g + b - 1)
                for k in range(H):
                    mm = wo_part(g, b, k)
                mm.then_inc(wo_mm, 1)

            def x2T_tile(src, dst):
                for k in range(H):
                    mm = pe.transpose(dst[:, k * P:(k + 1) * P], src[:, k * P:(k + 1) * P], ident[:])
                mm.then_inc(x2t_mm, 1)

            A_group(0)
            with pe.Fori(1, GROUPS - 1) as g:
                A_group(g)
            A_group(GROUPS - 1, before_last_w=first_O)
            zT_block(0, 0)
            zT_block(0, 1)
            pe.wait_ge(wo_ok, 2)

            def B_group(g):
                O_heads(g + 1, (0, 1))
                zT_block(g, 2)
                O_heads(g + 1, (2,))
                zT_block(g, 3)
                O_heads(g + 1, (3,))
                wo_first_tiles(g)
                wo_tile(g, 2)
                zT_block(g + 1, 0)
                zT_block(g + 1, 1)
                wo_tile(g, 3)

            B_group(0)
            with pe.Fori(1, GROUPS - 1) as g:
                B_group(g)
            zT_block(GROUPS - 1, 2)
            zT_block(GROUPS - 1, 3)
            wo_first_tiles(GROUPS - 1)
            wo_tile(GROUPS - 1, 2)
            for b in range(GB):
                pe.wait_ge(x2n_ok, b + 1)
                x2T_tile(x2n0_sb[:, b, :], bank(O_BANK0 + b))
            wo_tile(GROUPS - 1, 3)

            def product(dst, whi, wlo, mhi, mlo, start, stop, short):
                if short == "moving lo is zero":
                    pe.matmul(dst, whi, mhi, start=start, stop=False)
                    return pe.matmul(dst, wlo, mhi, start=False, stop=stop)
                if short:
                    pe.matmul(dst, whi, mhi, start=start, stop=False)
                    return pe.matmul(dst, whi, mlo, start=False, stop=stop)
                return three(dst, whi, wlo, mhi, mlo, start, stop)

            def gate_up(g, c, first=None, short=False):
                n = CH * g + c
                if c == 0:
                    pe.wait_ge(x2l_ok, GB * (g + 1))
                if c >= 2:
                    pe.wait_ge(hdl_ok, n - 1)
                if first:
                    pe.wait_ge(wffn_ok, c + 1)
                    if c == 1:
                        pe.wait_ge(x2_ok, B)
                for j, done in ((0, gate_mm), (1, up_mm)):
                    for k in range(H):
                        cols = slice(j * D + k * P, j * D + (k + 1) * P)
                        mm = product(bank(GU_BANKS[c % 2][j]), chunk_w(c, 0)[:, cols], chunk_w(c, 1)[:, cols],
                                   x2h_sb[:, k, :, :].rearrange("p b s -> p (b s)"),
                                   x2l_sb[:, k, :, :].rearrange("p b s -> p (b s)"),
                                   start=(k == 0), stop=(k == H - 1), short=short)
                    mm.then_inc(done, 1)

            def down(g, c, short=False):
                if c == 0:
                    pe.wait_ge(fin_ok, GB * g)
                pe.wait_ge(hdl_ok, CH * g + c + 1)
                for b in range(GB):
                    cols = slice(b * S, (b + 1) * S)
                    mm = product(bank(O_BANK0 + b), hd_sb[:, c % 2, 0, cols], hd_sb[:, c % 2, 1, cols],
                                 chunk_w(c, 0)[:, 2 * D:], chunk_w(c, 1)[:, 2 * D:],
                                 start=(c == 0), stop=(c == CH - 1),
                                 short="moving lo is zero" if short else False)
                    if c == CH - 1:
                        mm.then_inc(acc_mm, 1)
                if c < CH - 1:
                    mm.then_inc(down_mm, 1)

            def C_group(g, first=False, last=False, short=False):
                for c in range(CH):
                    gate_up(g, c, first, short)
                    if 0 < c < CH - 1:
                        down(g, c - 1, short)
                if not last:
                    for b in (0, 1):
                        if b == 0:
                            pe.wait_ge(hdl_ok, CH * g + CH - 1)
                        pe.wait_ge(x2n_ok, GB * (g + 1) + b + 1)
                        x2T_tile(x2n_sb[:, b, :], bank(GU_BANKS[1][b]))
                down(g, CH - 2, short)
                if not last:
                    for b in (2, 3):
                        if b == 2:
                            pe.wait_ge(hdl_ok, CH * g + CH)
                        pe.wait_ge(x2n_ok, GB * (g + 1) + b + 1)
                        x2T_tile(x2n_sb[:, b, :], bank(GU_BANKS[0][b - 2]))
                down(g, CH - 1, short)

            def C_other_groups(short):
                with pe.Fori(1, GROUPS - 1) as g:
                    C_group(g, short=short)
                C_group(GROUPS - 1, last=True, short=short)

            C_group(0, first=True)
            pe.wait_ge(flag_ok, 1)
            some_lo = pe.value_load(flag[0:1, 0:1], min_val=0, max_val=1)
            with pe.If(some_lo != 0):
                C_other_groups(short=False)
            with pe.Else():
                C_other_groups(short=True)

        @block.scalar
        def _(act):
            act.wait_ge(small_in, 16)
            nc.scalar.activation(tg[:], small[:, TG0:TG0 + 2], ACT.Tanh).then_inc(tanh_ok, 1)
            act.wait_ge(g_mm, 1)
            nc.scalar.activation(g_sb[:].rearrange("p h d -> p (h d)"), bank(T_BANKS[0]), ACT.Copy
                                 ).then_inc(g_ok, 1)

            def std_group(n, eps_col):
                act.wait_ge(mv_ok, GB * (n + 1))
                act.wait_ge(rstd_ok, n)
                nc.scalar.activation(std[:], mv[:, :, 1], ACT.Sqrt, bias=eps[:, eps_col:eps_col + 1]
                                     ).then_inc(std_ok, 1)

            def A_group(g, last=False):
                act.wait_ge(s_mm, g)
                for h in range(H):
                    act.wait_ge(t_mm, H * g + h + 1)
                    nc.scalar.activation(t_sb[:, h, :], bank(T_BANKS[h % 2]), ACT.Copy).then_inc(t_ok, 1)
                for b0 in (0, 2):
                    for b in (b0, b0 + 1):
                        act.wait_ge(v_mm, GB * g + b + 1)
                        src = bank(V_BANKS[b % 2]).rearrange("p (h e) -> p h e", h=H)
                        nc.scalar.activation(v_sb[:, :, g * GB + b, :], src, ACT.Copy).then_inc(v_ok, 1)
                    act.wait_ge(w_mm, H * g)
                    for b in (b0, b0 + 1):
                        act.wait_ge(xt_mm, GB * g + b + 1)
                        src = bank(X_BANKS[b]).rearrange("p (k s) -> p k s", k=H)
                        nc.scalar.activation(xT_sb[:, :, b, :], src, ACT.Copy).then_inc(xt_full, 1)
                        nc.scalar.activation(xTh_sb[:, :, b, :], src, ACT.Copy).then_inc(xt_hi, 1)
                if not last:
                    std_group(g + 1, 0)
                for e in range(H):
                    if last and e == 2:
                        std_group(GROUPS, 1)
                    act.wait_ge(w_mm, H * g + e + 1)
                    nc.scalar.activation(wT_sb[:, e, tokens(g)], bank(W_BANKS[e]), ACT.Relu
                                         ).then_inc(w_ok, 1)

            act.wait_ge(eps_ok, 2)
            std_group(0, 0)
            A_group(0)
            with act.Fori(1, GROUPS - 1) as g:
                A_group(g)
            A_group(GROUPS - 1, last=True)

            def y_block(g, k):
                act.wait_ge(zt_mm, H * g + k + 1)
                nc.scalar.activation(bank(Z_BANKS[k % 2]), bank(Z_BANKS[k % 2]), ACT.Identity,
                                     scale=small[:, GAM0 + k:GAM0 + k + 1],
                                     bias=small[:, BET0 + k:BET0 + k + 1]).then_inc(y_ok, 1)

            def wy_hi_block(g, k):
                act.wait_ge(wy_ok, H * g + k + 1)
                if k == 0:
                    act.wait_ge(wo_mm, GB * g)
                nc.scalar.activation(wy_hi[:, k, :, :].rearrange("p b s -> p (b s)"),
                                     bank(Z_BANKS[k % 2]), ACT.Copy).then_inc(wyh_ok, 1)

            def std2_tiles(first, n):
                act.wait_ge(mv2_ok, first + n)
                nc.scalar.activation(std2[:, first:first + n], l_mv[:, first:first + n, 1], ACT.Sqrt,
                                     bias=eps[:, 0:1]).then_inc(std2_ok, 1)

            def x2_hi(g, b, src):
                act.wait_ge(x2t_mm, GB * g + b + 1)
                nc.scalar.activation(x2h_sb[:, :, b, :], src.rearrange("p (k s) -> p k s", k=H), ACT.Copy
                                     ).then_inc(x2h_ok, 1)

            def wy_rest(g):
                wy_hi_block(g, 0)
                wy_hi_block(g, 1)
                y_block(g, 2)
                y_block(g, 3)
                wy_hi_block(g, 2)
                wy_hi_block(g, 3)

            def B_group(g):
                wy_rest(g)
                std_group(GROUPS + g + 1, 1)
                y_block(g + 1, 0)
                y_block(g + 1, 1)

            y_block(0, 0)
            y_block(0, 1)
            B_group(0)
            with act.Fori(1, GROUPS - 1) as g:
                B_group(g)
            wy_rest(GROUPS - 1)
            std2_tiles(0, GB)
            for b in range(GB):
                x2_hi(0, b, bank(O_BANK0 + b))

            def C_group(g, first=False, last=False):
                for c in range(CH):
                    n = CH * g + c
                    if first and c == 4:
                        std2_tiles(GB, B - GB)
                    act.wait_ge(gate_mm, n + 1)
                    if c >= 2:
                        act.wait_ge(hd_ok, n - 1)
                    nc.scalar.activation(silu_sb[:, c % 2, :], bank(GU_BANKS[c % 2][0]), ACT.Silu,
                                         scale=small[:, GS0 + c:GS0 + c + 1]).then_inc(silu_ok, 1)
                    act.wait_ge(hd_ok, n + 1)
                    if c >= 2:
                        act.wait_ge(down_mm, (CH - 1) * g + c - 1)
                    elif c == 0:
                        act.wait_ge(acc_mm, GB * g)
                    nc.scalar.activation(hd_sb[:, c % 2, 0, :], bank(GU_BANKS[c % 2][1]), ACT.Copy
                                         ).then_inc(hdh_ok, 1)
                if not last:
                    for b in range(GB):
                        x2_hi(g + 1, b, bank(GU_BANKS[1 - b // 2][b % 2]))

            C_group(0, first=True)
            with act.Fori(1, GROUPS - 1) as g:
                C_group(g)
            C_group(GROUPS - 1, last=True)

        @block.vector
        def _(dve):
            nc.vector.memset(eps[:, 0:1], LN_EPS).then_inc(eps_ok, 1)
            nc.vector.memset(eps[:, 1:2], GN_EPS).then_inc(eps_ok, 1)

            def standing():
                nc.vector.memset(carrier[:], 0.0)

            def x_norm(g):
                dve.wait_ge(x_in, 16 * (g + 1))
                standing()
                for b in range(GB):
                    nc.vector.bn_stats(st6[:, b, :], x_sb[:, g * GB + b, :])
                dve.drain()
                for b in range(GB):
                    nc.vector.bn_aggr(mv[:, b, :], st6[:, b, :]).then_inc(mv_ok, 1)
                dve.wait_ge(std_ok, g + 1)
                nc.vector.reciprocal(rstd[:], std[:]).then_inc(rstd_ok, 1)
                dve.wait_ge(rstd_ok, g + 1)
                dve.wait_ge(xt_mm, GB * g)
                for b in range(GB):
                    nc.vector.tensor_scalar(z_sb[:, b, :], x_sb[:, g * GB + b, :], mv[:, b, 0:1],
                                            rstd[:, b:b + 1], ALU.subtract, ALU.mult).then_inc(xn_ok, 1)

            def xT_lo(g):
                for b in range(GB):
                    dve.wait_ge(xt_hi, GB * g + b + 1)
                    nc.vector.tensor_tensor(
                        xTl_sb[:, :, b, :], bank(X_BANKS[b]).rearrange("p (k s) -> p k s", k=H),
                        xTh_sb[:, :, b, :].bitcast(F32), ALU.subtract).then_inc(xt_lo, 1)

            x_norm(0)
            with dve.Fori(0, GROUPS - 1) as g:
                xT_lo(g)
                x_norm(g + 1)
            xT_lo(GROUPS - 1)

            dve.wait_ge(s_mm, GROUPS)
            dve.wait_ge(mask_in, 16)
            nc.vector.tensor_tensor(aT_sb[:].rearrange("p h s -> p (h s)"), bank(S_BANK),
                                    mask_sb[:].rearrange("p h s -> p (h s)"), ALU.mult).then_inc(am_ok, 1)
            dve.wait_ge(am_ok, 1)
            flat = aT_sb[:].rearrange("p h s -> p (h s)")
            nc.vector.scalar_tensor_tensor(flat, flat, -1.0, flat, ALU.mult, ALU.max).then_inc(am_ok, 1)
            dve.wait_ge(am_ok, 2)
            nc.vector.tensor_scalar(flat, flat, 1.0, None, ALU.max).then_inc(a_ok, 1)

            def O_stats(g):
                dve.wait_ge(o_mm, g + 1)
                for b in range(GB):
                    nc.vector.bn_stats(st6[:, b, :], ps[:, O_BANK0:O_BANK0 + H, b * P:(b + 1) * P])
                dve.drain()
                for b in range(GB):
                    nc.vector.bn_aggr(mv[:, b, :], st6[:, b, :]).then_inc(mv_ok, 1)

            def O_rstd(g):
                dve.wait_ge(std_ok, GROUPS + g + 1)
                nc.vector.reciprocal(rstd[:], std[:]).then_inc(rstd_ok, 1)
                dve.wait_ge(rstd_ok, GROUPS + g + 1)
                dve.wait_ge(zt_mm, H * g)

            def O_norm(b):
                nc.vector.tensor_scalar(z_sb[:, b, :].rearrange("p (h e) -> p h e", h=H),
                                        ps[:, O_BANK0:O_BANK0 + H, b * P:(b + 1) * P],
                                        mv[:, b, 0:1], rstd[:, b:b + 1], ALU.subtract, ALU.mult
                                        ).then_inc(z_ok, 1)

            def wy_mul(g, k):
                dve.wait_ge(y_ok, H * g + k + 1)
                nc.vector.tensor_tensor(bank(Z_BANKS[k % 2]), bank(Z_BANKS[k % 2]),
                                        wT_sb[:, k, tokens(g)], ALU.mult).then_inc(wy_ok, 1)

            def wy_lo_block(g, k):
                dve.wait_ge(wyh_ok, H * g + k + 1)
                nc.vector.tensor_tensor(wy_lo[:, k, :, :].rearrange("p b s -> p (b s)"),
                                        bank(Z_BANKS[k % 2]),
                                        wy_hi[:, k, :, :].rearrange("p b s -> p (b s)").bitcast(F32),
                                        ALU.subtract).then_inc(wyl_ok, 1)

            def wy_rest(g):
                wy_lo_block(g, 0)
                wy_lo_block(g, 1)
                wy_mul(g, 2)
                wy_mul(g, 3)
                wy_lo_block(g, 2)
                wy_lo_block(g, 3)

            def residual(g, b):
                t = g * GB + b
                dve.wait_ge(wo_mm, t + 1)
                nc.vector.scalar_tensor_tensor(x_sb[:, t, :], bank(WO_BANKS[b % 2]), tg[:, 0:1],
                                               x_sb[:, t, :], ALU.mult, ALU.add).then_inc(x2_ok, 1)

            def x2_stats(g):
                dve.wait_ge(x2_ok, GB * (g + 1))
                for b in range(GB):
                    t = g * GB + b
                    nc.vector.bn_stats(l_st6[:, t, :], x_sb[:, t, :])
                dve.drain()
                for b in range(GB):
                    t = g * GB + b
                    nc.vector.bn_aggr(l_mv[:, t, :], l_st6[:, t, :]).then_inc(mv2_ok, 1)

            def x2_rstd(n, first, count):
                dve.wait_ge(std2_ok, n)
                nc.vector.reciprocal(rstd2[:, first:first + count], std2[:, first:first + count]
                                     ).then_inc(rstd2_ok, 1)

            def x2_norm(dst, g, b):
                t = g * GB + b
                nc.vector.tensor_scalar(dst[:, b, :], x_sb[:, t, :], l_mv[:, t, 0:1], rstd2[:, bass.ds(t, 1)],
                                        ALU.subtract, ALU.mult).then_inc(x2n_ok, 1)

            def x2_lo(g, b, src):
                dve.wait_ge(x2h_ok, GB * g + b + 1)
                nc.vector.tensor_tensor(x2l_sb[:, :, b, :], src.rearrange("p (k s) -> p k s", k=H),
                                        x2h_sb[:, :, b, :].bitcast(F32), ALU.subtract).then_inc(x2l_ok, 1)

            O_stats(0)
            O_rstd(0)
            for b in range(GB):
                O_norm(b)
            dve.wait_ge(ds_in, 16)
            nc.vector.tensor_scalar(dsg_sb[:], dsg_sb[:], tg[:, 1:2], None, ALU.mult).then_inc(dsg_ok, 1)
            def B_group(g):
                wy_rest(g)
                O_stats(g + 1)
                residual(g, 0)
                O_rstd(g + 1)
                for b in range(GB):
                    O_norm(b)
                residual(g, 1)
                residual(g, 2)
                wy_mul(g + 1, 0)
                wy_mul(g + 1, 1)
                residual(g, 3)

            wy_mul(0, 0)
            wy_mul(0, 1)
            B_group(0)
            with dve.Fori(1, GROUPS - 1) as g:
                B_group(g)
            wy_rest(GROUPS - 1)
            x2_stats(0)
            residual(GROUPS - 1, 0)
            x2_rstd(1, 0, GB)
            dve.wait_ge(rstd2_ok, 1)
            x2_norm(x2n0_sb, 0, 0)
            x2_norm(x2n0_sb, 0, 1)
            residual(GROUPS - 1, 1)
            x2_norm(x2n0_sb, 0, 2)
            x2_norm(x2n0_sb, 0, 3)
            residual(GROUPS - 1, 2)
            for b in range(GB):
                x2_lo(0, b, bank(O_BANK0 + b))
            residual(GROUPS - 1, 3)

            def C_group(g, first=False, last=False):
                for c in range(CH):
                    n = CH * g + c
                    dve.wait_ge(silu_ok, n + 1)
                    dve.wait_ge(up_mm, n + 1)
                    u = bank(GU_BANKS[c % 2][1])
                    nc.vector.scalar_tensor_tensor(u, u, small[:, US0 + c:US0 + c + 1], silu_sb[:, c % 2, :],
                                                   ALU.mult, ALU.mult).then_inc(hd_ok, 1)
                    dve.wait_ge(hdh_ok, n + 1)
                    nc.vector.tensor_tensor(hd_sb[:, c % 2, 1, :], u, hd_sb[:, c % 2, 0, :].bitcast(F32),
                                            ALU.subtract).then_inc(hdl_ok, 1)
                    if first:
                        dve.wait_ge(wffn_ok, c + 1)
                        nc.vector.tensor_reduce(lomax[:, c:c + 1], chunk_w(c, 1).bitcast(F32), AX_X, ALU.max,
                                                apply_absolute_value=True).then_inc(lomax_ok, 1)
                    if first and 1 <= c < GROUPS:
                        x2_stats(c)
                    if first and c == GROUPS:
                        x2_rstd(2, GB, B - GB)
                    if not last and 5 <= c < 5 + GB:
                        if c == 5:
                            dve.wait_ge(x2t_mm, GB * (g + 1))
                            dve.wait_ge(rstd2_ok, 2)
                        x2_norm(x2n_sb, g + 1, c - 5)
                if not last:
                    for b in range(GB):
                        x2_lo(g + 1, b, bank(GU_BANKS[1 - b // 2][b % 2]))
                if first:
                    dve.wait_ge(lomax_ok, CH)
                    nc.vector.tensor_reduce(lomax[:, CH:], lomax[:, 0:CH], AX_X, ALU.max).then_inc(loany_ok, 1)
                    dve.wait_ge(loall_ok, 1)
                    nc.vector.tensor_scalar(flag[:], loall[:], 0.0, None, ALU.not_equal).then_inc(flag_ok, 1)
                for b in range(GB):
                    t = g * GB + b
                    dve.wait_ge(acc_mm, t + 1)
                    acc = bank(O_BANK0 + b)
                    nc.vector.tensor_tensor(acc, acc, dsg_sb[:], ALU.mult).then_inc(sc_ok, 1)
                    dve.wait_ge(sc_ok, t + 1)
                    nc.vector.tensor_tensor(x_sb[:, t, :], acc, x_sb[:, t, :], ALU.add).then_inc(fin_ok, 1)

            C_group(0, first=True)
            with dve.Fori(1, GROUPS - 1) as g:
                C_group(g)
            C_group(GROUPS - 1, last=True)


def decay_mask():
    gam = (1.0 - 2.0 ** (-5.0 - np.arange(H, dtype=np.float32))).astype(np.float32)
    idx = np.arange(S, dtype=np.float32)
    expo = idx[None, :] - idx[:, None]
    d = np.where(expo[None] <= 0, gam[:, None, None] ** expo[None], np.float32(0))
    d = d / np.sqrt(d.sum(axis=-1))[:, None, :] / np.sqrt(np.float32(P))
    return np.ascontiguousarray(d.transpose(2, 0, 1).astype(np.float32))


def kernel(**inputs):
    import concourse.bacc as bacc
    from concourse.bass_utils import run_bass_kernel_spmd

    a = {n: np.asarray(v) for n, v in inputs.items()}

    def rows(w):
        return w.reshape(-1, P, w.shape[-1]).transpose(1, 0, 2)

    def up_cols(w):
        return w.reshape(CH, P, H, P).transpose(0, 3, 2, 1).reshape(CH, P, D)

    Wh = a["L0_xattn_Wh"]
    data = {
        "x": a["x"],
        "ctxT": a["ctx_2048"].reshape(GROUPS, GB, S, H, P).transpose(0, 4, 3, 1, 2).reshape(GROUPS, P, H, NT),
        "WhT": Wh.transpose(2, 0, 1),
        "Wh": Wh.transpose(1, 0, 2),
        "wg": rows(a["L0_xattn_wg_w"]),
        "wo": rows(a["L0_xattn_wo_w"]),
        "wffn": np.concatenate([up_cols(a["L0_ffn_gate_w"]), up_cols(a["L0_ffn_up_w"]),
                                a["L0_ffn_down_w"].T.reshape(CH, P, D)], axis=2),
        "smalls": np.concatenate(
            [a["L0_ffn_gate_s"].reshape(CH, P).T, a["L0_ffn_up_s"].reshape(CH, P).T,
             a["L0_xattn_gn_gamma"].reshape(H, P).T, a["L0_xattn_gn_beta"].reshape(H, P).T,
             np.broadcast_to(a["g_xattn"].reshape(1, 1), (P, 1)),
             np.broadcast_to(a["g_ffn"].reshape(1, 1), (P, 1))], axis=1),
        "down_s": a["L0_ffn_down_s"].reshape(1, D),
        "mask": decay_mask(),
    }
    nc = bacc.Bacc("TRN2", target_bir_lowering=False, num_devices=1)
    arrays, args = {}, []
    for name, v in data.items():
        v = np.ascontiguousarray(v)
        arrays[f"in_{name}"] = v
        args.append(nc.dram_tensor(f"in_{name}", v.shape, mybir.dt.from_np(v.dtype), kind="ExternalInput").ap())
    args.append(nc.dram_tensor("out_x", (B, S, D), F32, kind="ExternalOutput").ap())
    build(nc, *args)
    r = run_bass_kernel_spmd(nc, [arrays], core_ids=[0])
    return r.results[0]["out_x"]
```

```python
from contextlib import ExitStack

import numpy as np

import concourse.bass as bass
from concourse import mybir

F32 = mybir.dt.float32
F32R = mybir.dt.float32r
ALU = mybir.AluOpType
ACT = mybir.ActivationFunctionType
AX_X = mybir.AxisListType.X

P = 128
B, S, D = 16, 128, 512
H = D // P
INTER = 1408
CH = INTER // P
GB = 4
GROUPS = B // GB
NT = GB * S
LN_EPS = 1e-5
GN_EPS = 1e-3

S_BANK = 0
G_BANKS = (3, 4, 5, 6)
T_BANKS = (1, 2)
X_BANKS = (3, 4, 1, 2)
V_BANKS = (5, 6)
W_BANKS = (7, 5, 6, 7)
O_BANK0 = 1
Z_BANKS = (5, 6)
WO_BANKS = (7, 0)
GU_BANKS = ((5, 6), (7, 0))

GS0, US0, GAM0, BET0, TG0 = 0, CH, 2 * CH, 2 * CH + H, 2 * CH + 2 * H
N_SMALL = TG0 + 2
WROW = 3 * D
EARLY, MID, LATE = range(0, 4), range(4, 9), range(9, CH)
V_CHUNKS = 2
AHEAD = len(EARLY)

KB = 1024


def build(nc, x, ctxT, WhT, Wh, wg, wo, wffn, smalls, down_s, mask, out):
    base = -(-nc.sbuf_base // 64) * 64
    with ExitStack() as ctx:
        def at(name, offset, shape, dt=F32):
            return nc.alloc_sbuf_tensor_at(name, [P] + shape, dt, offset=base + int(offset))

        def sem(name):
            return ctx.enter_context(nc.semaphore(name))

        x_sb = at("x_sb", 0, [B, D])
        v_sb = at("v_sb", 32 * KB, [H, B, P])
        wT_sb = at("wT_sb", 64 * KB, [H, B * S])
        ctx_sb = at("ctx_sb", 96 * KB, [H, NT])
        t_sb = at("t_sb", 112 * KB, [H, NT])
        xT_sb = at("xT_sb", 120 * KB, [H, GB, S])
        xTh_sb = at("xTh_sb", 128 * KB, [H, GB, S], F32R)
        xTl_sb = at("xTl_sb", 136 * KB, [H, GB, S], F32R)
        wg_hi = at("wg_hi", 144 * KB, [H, H, P], F32R)
        wg_raw = at("wg_raw", 152 * KB, [H, H, P])
        wg_lo = at("wg_lo", 152 * KB, [H, H, P], F32R)
        wh_sb = at("wh_sb", 160 * KB, [H, P])
        whT_sb = at("whT_sb", 162 * KB, [H, P])
        g_sb = at("g_sb", 164 * KB, [H, P])
        mask_sb = at("mask_sb", 166 * KB, [H, P])
        ctx_hi = at("ctx_hi", 168 * KB, [H, NT], F32R)
        ctx_lo = at("ctx_lo", 176 * KB, [H, NT], F32R)
        g_hi = at("g_hi", 192 * KB, [H, P], F32R)
        g_lo = at("g_lo", 194 * KB, [H, P], F32R)
        wy_hi = at("wy_hi", 144 * KB, [H, GB, S], F32R)
        wy_lo = at("wy_lo", 152 * KB, [H, GB, S], F32R)
        v_hi = at("v_hi", 160 * KB, [H, GB, P], F32R)
        v_lo = at("v_lo", 32 * KB, [H, B, P], F32R)
        x2n0_sb = at("x2n0_sb", 160 * KB, [GB, D])
        w_early = at("w_early", 96 * KB, [len(EARLY), 2, WROW], F32R)
        w_mid = at("w_mid", 32 * KB, [len(MID), 2, WROW], F32R)
        w_late = at("w_late", 144 * KB, [len(LATE), 2, WROW], F32R)
        w_early_raw = at("w_early_raw", 96 * KB, [len(EARLY), 2, WROW])
        w_mid_raw = at("w_mid_raw", 32 * KB, [len(MID), 2, WROW])
        w_late_raw = at("w_late_raw", 144 * KB, [len(LATE), 2, WROW])
        silu_sb = at("silu_sb", 92 * KB, [2, NT])
        wo_hi = at("wo_hi", 168 * KB, [H, D], F32R)
        wo_raw = at("wo_raw", 176 * KB, [H, D])
        wo_lo = at("wo_lo", 176 * KB, [H, D], F32R)
        hd_sb = at("hd_sb", 168 * KB, [2, 2, NT], F32R)
        junk_B = at("junk_B", 192 * KB, [WROW])
        junk_C = at("junk_C", 176 * KB, [WROW])
        x2n_sb = at("x2n_sb", 176 * KB, [GB, D])
        sum_sb = at("sum_sb", 176 * KB, [GB, D])
        z_sb = at("z_sb", 184 * KB, [GB, D])
        x2h_sb = at("x2h_sb", 184 * KB, [H, GB, S], F32R)
        x2l_sb = at("x2l_sb", 192 * KB, [H, GB, S], F32R)
        a_hi = at("a_hi", 198 * KB, [H, P], F32R)
        top = 200 * KB
        a_lo = at("a_lo", top, [H, P], F32R)
        aT_sb = at("aT_sb", top, [H, P])
        dsg_sb = at("dsg_sb", top + 2 * KB, [D])
        ident = at("ident", top + 4 * KB, [P])
        zero_sb = at("zero_sb", top + 4.5 * KB, [P])
        small = at("small", top + 5 * KB, [N_SMALL])
        tg = at("tg", top + 5.25 * KB, [2])
        eps = at("eps", top + 5.3125 * KB, [2])
        st6 = at("st6", top + 5.375 * KB, [GB, 6])
        mv = at("mv", top + 5.5 * KB, [GB, 2])
        std = at("std", top + 5.5625 * KB, [GB])
        rstd = at("rstd", top + 5.625 * KB, [GB])
        l_st6 = at("l_st6", top + 5.75 * KB, [B, 6])
        l_mv = at("l_mv", top + 6.125 * KB, [B, 2])
        std2 = at("std2", top + 6.25 * KB, [B])
        losum = at("losum", top + 6.5 * KB, [CH])
        locum = at("locum", top + 6.5625 * KB, [CH + 1])
        loall = at("loall", top + 6.625 * KB, [CH])
        flag = at("flag", top + 6.6875 * KB, [CH], mybir.dt.int32)
        carrier = at("carrier", top + 6.375 * KB, [1])
        rstd2 = at("rstd2", top + 6.3125 * KB, [B])

        ps = ctx.enter_context(nc.psum_tensor("ps", [P, 8, 512], F32))

        whT_in, wh_in, small_in, mask_in = sem("whT_in"), sem("wh_in"), sem("small_in"), sem("mask_in")
        wg_in, wo_in, ds_in = sem("wg_in"), sem("wo_in"), sem("ds_in")
        ctx0_in = [sem(f"ctx0_in{i}") for i in range(2)]
        x0_in = [sem(f"x0_in{i}") for i in range(2)]
        x_in, ctx_in = sem("x_in"), sem("ctx_in")
        wffn_in = sem("wffn_in")
        ident_ok, zero_ok, eps_ok = sem("ident_ok"), sem("zero_ok"), sem("eps_ok")
        id0 = sem("id0")
        wg_hi_ok, wg_ok = sem("wg_hi_ok"), sem("wg_ok")
        wo_hi_ok, wo_ok = sem("wo_hi_ok"), sem("wo_ok")
        wffn_hi, wffn_ok = sem("wffn_hi"), sem("wffn_ok")
        table_ok = sem("table_ok")
        tanh_ok, dsg_ok = sem("tanh_ok"), sem("dsg_ok")
        g_mm, g_ok = sem("g_mm"), sem("g_ok")
        g_hi_ok, g_lo_ok = sem("g_hi_ok"), sem("g_lo_ok")
        ctx_hi_ok, ctx_lo_ok = sem("ctx_hi_ok"), sem("ctx_lo_ok")
        st_ok, mv_ok = sem("st_ok"), sem("mv_ok")
        std_ok, rstd_ok = sem("std_ok"), sem("rstd_ok")
        xn_ok, xt_mm = sem("xn_ok"), sem("xt_mm")
        xt_full, xt_hi, xt_lo = sem("xt_full"), sem("xt_hi"), sem("xt_lo")
        t_mm, t_ok = sem("t_mm"), sem("t_ok")
        v_mm, v_ok = sem("v_mm"), sem("v_ok")
        s_mm = sem("s_mm")
        w_mm, w_ok = sem("w_mm"), sem("w_ok")
        am_ok, a_ok = sem("am_ok"), sem("a_ok")
        a_hi_ok, a_lo_ok = sem("a_hi_ok"), sem("a_lo_ok")
        v_hi_ok, v_lo_ok = sem("v_hi_ok"), sem("v_lo_ok")
        o_mm, z_ok = sem("o_mm"), sem("z_ok")
        zt_mm, y_ok, wy_ok, wyh_ok, wyl_ok = (
            sem("zt_mm"), sem("y_ok"), sem("wy_ok"), sem("wyh_ok"), sem("wyl_ok"))
        wo_mm, x2_ok = sem("wo_mm"), sem("x2_ok")
        lst_ok, mv2_ok = sem("lst_ok"), sem("mv2_ok")
        wo_half = sem("wo_half")
        std2_ok, rstd2_ok = sem("std2_ok"), sem("rstd2_ok")
        x2n_ok, x2t_mm, x2h_ok, x2l_ok = (
            sem("x2n_ok"), sem("x2t_mm"), sem("x2h_ok"), sem("x2l_ok"))
        gate_mm, up_mm, silu_ok = sem("gate_mm"), sem("up_mm"), sem("silu_ok")
        hd_ok, hdh_ok, hdl_ok, down_mm = sem("hd_ok"), sem("hdh_ok"), sem("hdl_ok"), sem("down_mm")
        acc_mm, sc_ok = sem("acc_mm"), sem("sc_ok")
        fin_ok, fin_dve = sem("fin_ok"), sem("fin_dve")
        stored = sem("stored")
        losum_ok, locum_ok, loall_ok, flag_ok = (
            sem("losum_ok"), sem("locum_ok"), sem("loall_ok"), sem("flag_ok"))

        def bank(i):
            return ps[:, i, :]

        def tiles(g):
            return bass.ds(g * GB, GB)

        def tokens(g):
            return bass.ds(g * NT, NT)

        def chunk_of(c, early, mid, late, part):
            for chunks, tensor in ((EARLY, early), (MID, mid), (LATE, late)):
                if c in chunks:
                    return tensor[:, c - chunks[0], part, :]

        def chunk_w(c, part):
            return chunk_of(c, w_early, w_mid, w_late, part)

        def chunk_raw(c):
            return chunk_of(c, w_early_raw, w_mid_raw, w_late_raw, 1)

        block = ctx.enter_context(nc.Block())

        @block.sync
        def _(sp):
            sp.dma_start(whT_sb[:], WhT).then_inc(whT_in, 16)
            sp.dma_start(small[:], smalls).then_inc(small_in, 16)
            for i in range(2):
                heads = slice(2 * i, 2 * i + 2)
                sp.dma_start(ctx_sb[:, heads, :], ctxT[0, :, heads, :]).then_inc(ctx0_in[i], 16)
            for i in range(2):
                b = slice(2 * i, 2 * i + 2)
                sp.dma_start(x_sb[:, b, :], x[b].rearrange("b s d -> s b d")).then_inc(x0_in[i], 16)
                if i == 0:
                    sp.dma_start(wh_sb[:], Wh).then_inc(wh_in, 16)
            sp.dma_start(wg_raw[:], wg).then_inc(wg_in, 16)

            def load_x(g):
                sp.dma_start(x_sb[:, tiles(g), :], x[tiles(g)].rearrange("b s d -> s b d")).then_inc(x_in, 16)

            def load_ctx(g):
                sp.wait_ge(v_mm, GB * g)
                sp.dma_start(ctx_sb[:], ctxT[bass.ds(g, 1)].rearrange("g p h n -> (g p) h n")
                             ).then_inc(ctx_in, 16)

            load_x(1)
            load_ctx(1)
            sp.dma_start(mask_sb[:], mask).then_inc(mask_in, 16)
            sp.dma_start(dsg_sb[:], down_s.to_broadcast([P, D])).then_inc(ds_in, 16)
            with sp.Fori(2, GROUPS) as g:
                sp.wait_ge(x_in, 16 * (g - 1))
                load_x(g)
                sp.wait_ge(ctx_in, 16 * (g - 1))
                load_ctx(g)

            sp.wait_ge(t_mm, H * GROUPS)
            sp.dma_start(wo_raw[:], wo).then_inc(wo_in, 16)
            sp.wait_ge(w_mm, H * GROUPS)
            sp.wait_ge(xt_lo, B)
            sp.dma_start(w_early_raw[:, 0, 1, :], wffn[0]).then_inc(wffn_in, 16)
            with sp.Fori(1, len(EARLY)) as c:
                sp.wait_ge(wffn_in, 16 * c)
                sp.dma_start(w_early_raw[:, bass.ds(c, 1), 1, :],
                             wffn[bass.ds(c, 1)].rearrange("c p n -> p c n")).then_inc(wffn_in, 16)

            def mid(first, last):
                with sp.Fori(first, last) as c:
                    sp.wait_ge(wffn_in, 16 * c)
                    sp.dma_start(w_mid_raw[:, bass.ds(c - MID[0], 1), 1, :],
                                 wffn[bass.ds(c, 1)].rearrange("c p n -> p c n")).then_inc(wffn_in, 16)

            sp.wait_ge(o_mm, GROUPS)
            mid(MID[0], MID[V_CHUNKS])
            sp.wait_ge(wy_ok, H * GROUPS)
            mid(MID[V_CHUNKS], LATE[0])
            sp.wait_ge(wo_mm, B)
            sp.wait_ge(x2t_mm, GB)
            for c in LATE:
                sp.wait_ge(wffn_in, 16 * c)
                sp.dma_start(w_late_raw[:, c - LATE[0], 1, :], wffn[c]).then_inc(wffn_in, 16)
            with sp.Fori(0, B - GB) as t:
                sp.wait_ge(fin_ok, t + 1)
                sp.dma_start(out[bass.ds(t, 1)].rearrange("b s d -> s b d"),
                             x_sb[:, bass.ds(t, 1), :]).then_inc(stored, 16)
            for b, done, count in ((0, fin_dve, 1), (1, fin_ok, B - GB + 1), (3, fin_dve, 2),
                                   (2, fin_ok, B - GB + 2)):
                sp.wait_ge(done, count)
                sp.dma_start(out[B - GB + b], x_sb[:, B - GB + b, :]).then_inc(stored, 16)
            sp.wait_ge(stored, 16 * B)

        @block.gpsimd
        def _(pool):
            nc.gpsimd.memset(zero_sb[:], 0.0).then_inc(zero_ok, 1)
            nc.gpsimd.memset(ident[:], 0.0).then_inc(id0, 1)
            pool.wait_ge(id0, 1)
            nc.gpsimd.affine_select(out=ident[:], in_=ident[:], compare_op=ALU.not_equal, fill=1.0,
                                    base=0, pattern=[[-1, P]], channel_multiplier=1
                                    ).then_inc(ident_ok, 1)
            nc.gpsimd.memset(locum[:, 0:1], 0.0).then_inc(locum_ok, 1)
            for e in range(H):
                pool.wait_ge(wg_hi_ok, e + 1)
                nc.gpsimd.tensor_tensor(wg_lo[:, e], wg_raw[:, e], wg_hi[:, e].bitcast(F32), ALU.subtract
                                        ).then_inc(wg_ok, 1)
            pool.wait_ge(g_hi_ok, 1)
            nc.gpsimd.tensor_tensor(g_lo[:], g_sb[:], g_hi[:].bitcast(F32), ALU.subtract).then_inc(g_lo_ok, 1)
            with pool.Fori(1, GROUPS) as g:
                for h in range(H):
                    pool.wait_ge(ctx_hi_ok, H * (g - 1) + h + 1)
                    nc.gpsimd.tensor_tensor(ctx_lo[:, h], ctx_sb[:, h], ctx_hi[:, h].bitcast(F32),
                                            ALU.subtract).then_inc(ctx_lo_ok, 1)
            for k in range(H):
                pool.wait_ge(wo_hi_ok, k + 1)
                nc.gpsimd.tensor_tensor(wo_lo[:, k], wo_raw[:, k], wo_hi[:, k].bitcast(F32), ALU.subtract
                                        ).then_inc(wo_ok, 1)

            def flag_of(c):
                pool.wait_ge(losum_ok, c + 1)
                pool.wait_ge(locum_ok, c + 1)
                nc.gpsimd.tensor_tensor(locum[:, c + 1:c + 2], locum[:, c:c + 1], losum[:, c:c + 1], ALU.add
                                        ).then_inc(locum_ok, 1)
                pool.wait_ge(locum_ok, c + 2)
                nc.gpsimd.partition_all_reduce(loall[:, c:c + 1], locum[:, c + 1:c + 2], P,
                                               bass.bass_isa.ReduceOp.add).then_inc(loall_ok, 1)
                pool.wait_ge(loall_ok, c + 1)
                nc.gpsimd.tensor_scalar(flag[:, c:c + 1], loall[:, c:c + 1], 0.0, None, ALU.is_gt
                                        ).then_inc(flag_ok, 1)

            def v_lo_part(g):
                for h in range(H):
                    pool.wait_ge(v_hi_ok, H * (g - 1) + h + 1)
                    nc.gpsimd.tensor_tensor(v_lo[:, h, tiles(g), :], v_sb[:, h, tiles(g), :],
                                            v_hi[:, h].bitcast(F32), ALU.subtract).then_inc(v_lo_ok, 1)

            pool.wait_ge(a_hi_ok, 1)
            pool.wait_ge(o_mm, 1)
            nc.gpsimd.tensor_tensor(a_lo[:], aT_sb[:], a_hi[:].bitcast(F32), ALU.subtract
                                    ).then_inc(a_lo_ok, 1)
            v_lo_part(1)
            for c in range(CH):
                if c + 2 < GROUPS:
                    v_lo_part(c + 2)
                pool.wait_ge(wffn_hi, c + 1)
                nc.gpsimd.tensor_tensor(chunk_w(c, 1), chunk_raw(c), chunk_w(c, 0).bitcast(F32), ALU.subtract
                                        ).then_inc(wffn_ok, 1)
                if c:
                    flag_of(c - 1)
            flag_of(CH - 1)

            for t in [*range(B - GB), B - GB + 1, B - GB + 2]:
                pool.wait_ge(sc_ok, t + 1)
                nc.gpsimd.tensor_tensor(x_sb[:, t, :], sum_sb[:, t % GB, :], x_sb[:, t, :], ALU.add
                                        ).then_inc(fin_ok, 1)

        @block.tensor
        def _(pe):
            def three(dst, whi, wlo, mhi, mlo, start, stop):
                pe.matmul(dst, whi, mhi, start=start, stop=False)
                pe.matmul(dst, whi, mlo, start=False, stop=False)
                return pe.matmul(dst, wlo, mhi, start=False, stop=stop)

            pe.wait_ge(zero_ok, 1)
            for h in range(H):
                pe.matmul(bank(S_BANK)[:, h * P:(h + 1) * P], zero_sb[:], zero_sb[:], start=True, stop=True)
            pe.wait_ge(whT_in, 16)
            for h in range(H):
                pe.matmul(bank(G_BANKS[h])[:, 0:P], whT_sb[:, h, :], whT_sb[:, h, :],
                          start=True, stop=True).then_inc(g_mm, 1)
            pe.wait_ge(ident_ok, 1)

            def V_tile(g, b):
                if b >= 2:
                    pe.wait_ge(v_ok, GB * g + b - 1)
                for h in range(H):
                    mm = pe.matmul(bank(V_BANKS[b % 2])[:, h * P:(h + 1) * P],
                                   ctx_sb[:, h, b * S:(b + 1) * S], wh_sb[:, h, :],
                                   start=True, stop=True)
                mm.then_inc(v_mm, 1)

            def xT_tile(g, b):
                pe.wait_ge(xn_ok, GB * g + b + 1)
                if b == 2:
                    pe.wait_ge(t_ok, H * (g + 1))
                for k in range(H):
                    mm = pe.transpose(bank(X_BANKS[b])[:, k * P:(k + 1) * P],
                                      z_sb[:, b, k * P:(k + 1) * P], ident[:])
                mm.then_inc(xt_mm, 1)

            def A_group(g, first=False, before_last_w=None):
                if not first:
                    pe.wait_ge(ctx_in, 16 * g)
                    pe.wait_ge(g_lo_ok, 1)
                    pe.wait_ge(xt_lo, GB * g)
                for h in range(H):
                    if first:
                        pe.wait_ge(g_ok, h + 1)
                        pe.wait_ge(ctx0_in[h // 2], 16)
                    if h >= 2:
                        pe.wait_ge(t_ok, H * g + h - 1)
                    if first:
                        mm = pe.matmul(bank(T_BANKS[h % 2]), g_sb[:, h, :], ctx_sb[:, h, :],
                                       start=True, stop=True)
                    else:
                        pe.wait_ge(ctx_lo_ok, H * (g - 1) + h + 1)
                        mm = three(bank(T_BANKS[h % 2]), g_hi[:, h, :], g_lo[:, h, :],
                                   ctx_hi[:, h, :], ctx_lo[:, h, :], start=True, stop=True)
                    mm.then_inc(t_mm, 1)
                pe.wait_ge(wh_in, 16)
                pe.wait_ge(w_ok, H * g)
                if first:
                    for b in range(GB):
                        V_tile(g, b)
                    for b in range(GB):
                        xT_tile(g, b)
                else:
                    for b0 in (0, 2):
                        V_tile(g, b0)
                        V_tile(g, b0 + 1)
                        xT_tile(g, b0)
                        xT_tile(g, b0 + 1)
                pe.wait_ge(t_ok, H * (g + 1))
                for b in range(GB):
                    pe.wait_ge(xt_full, GB * g + b + 1)
                    for h in range(H):
                        mm = pe.matmul(bank(S_BANK)[:, h * P:(h + 1) * P],
                                       t_sb[:, h, b * S:(b + 1) * S], xT_sb[:, h, b, :],
                                       start=False, stop=True, skip_group_check=True)
                mm.then_inc(s_mm, 1)
                pe.wait_ge(xt_lo, GB * (g + 1))
                for e in range(H):
                    if first:
                        pe.wait_ge(wg_ok, e + 1)
                    if e == 1 and before_last_w:
                        before_last_w()
                    if e == 1:
                        pe.wait_ge(v_ok, GB * (g + 1))
                    if e == 3:
                        pe.wait_ge(w_ok, H * g + 1)
                    for k in range(H):
                        mm = three(bank(W_BANKS[e]), wg_hi[:, e, k, :], wg_lo[:, e, k, :],
                                   xTh_sb[:, k, :, :].rearrange("p b s -> p (b s)"),
                                   xTl_sb[:, k, :, :].rearrange("p b s -> p (b s)"),
                                   start=(k == 0), stop=(k == H - 1))
                    mm.then_inc(w_mm, 1)

            def ahead_of_first(g):
                return not (isinstance(g, int) and g == 0)

            def O_heads(g, heads):
                for h in heads:
                    if ahead_of_first(g):
                        pe.wait_ge(v_lo_ok, H * (g - 1) + h + 1)
                        mm = three(bank(O_BANK0 + h), a_hi[:, h, :], a_lo[:, h, :],
                                   v_hi[:, h].rearrange("p b e -> p (b e)"), v_lo[:, h, tiles(g), :],
                                   start=True, stop=True)
                    else:
                        mm = pe.matmul(bank(O_BANK0 + h), aT_sb[:, h, :], v_sb[:, h, tiles(g), :],
                                       start=True, stop=True)
                if h == H - 1:
                    mm.then_inc(o_mm, 1)

            def first_O():
                pe.wait_ge(a_ok, 1)
                pe.wait_ge(t_ok, H * GROUPS)
                pe.wait_ge(xt_lo, B)
                O_heads(0, range(H))

            def zT_block(g, k):
                if k == 0:
                    pe.wait_ge(z_ok, GB * (g + 1))
                if k < 2 and not ahead_of_first(g):
                    pe.wait_ge(w_ok, H * (GROUPS - 1) + k + 2)
                if k >= 2:
                    pe.wait_ge(wyl_ok, H * g + k - 1)
                elif ahead_of_first(g):
                    pe.wait_ge(wyl_ok, H * g + k - 1)
                for b in range(GB):
                    mm = pe.transpose(bank(Z_BANKS[k % 2])[:, b * S:(b + 1) * S],
                                      z_sb[:, b, k * P:(k + 1) * P], ident[:])
                mm.then_inc(zt_mm, 1)

            def wo_part(g, b, k):
                pe.wait_ge(wyl_ok, H * g + k + 1)
                return three(bank(WO_BANKS[b % 2]), wy_hi[:, k, b, :], wy_lo[:, k, b, :],
                             wo_hi[:, k, :], wo_lo[:, k, :], start=(k == 0), stop=(k == H - 1))

            def wo_first_tiles(g):
                pe.wait_ge(x2_ok, GB * g)
                for k0 in (0, 2):
                    for b in (0, 1):
                        for k in (k0, k0 + 1):
                            mm = wo_part(g, b, k)
                        if k0 == 2:
                            mm.then_inc(wo_mm, 1)

            def wo_tile(g, b, blocks=range(H)):
                if blocks[0] == 0:
                    pe.wait_ge(x2_ok, GB * g + b - 1)
                for k in blocks:
                    mm = wo_part(g, b, k)
                mm.then_inc(wo_mm if blocks[-1] == H - 1 else wo_half, 1)

            def x2T_tile(src, dst):
                for k in range(H):
                    mm = pe.transpose(dst[:, k * P:(k + 1) * P], src[:, k * P:(k + 1) * P], ident[:])
                mm.then_inc(x2t_mm, 1)

            A_group(0, first=True)
            with pe.Fori(1, GROUPS - 1) as g:
                A_group(g)
            A_group(GROUPS - 1, before_last_w=first_O)
            def B_group(g, first=False, last=False, hold=False):
                zT_block(g, 0)
                zT_block(g, 1)
                if last:
                    wo_tile(g - 1, 3, (2, 3))
                else:
                    pe.wait_ge(a_lo_ok, 1)
                    O_heads(g + 1, range(H))
                if first:
                    pe.wait_ge(wo_ok, H)
                    pe.wait_ge(w_ok, H * GROUPS)
                zT_block(g, 2)
                zT_block(g, 3)
                wo_first_tiles(g)
                wo_tile(g, 2)
                if last:
                    for b in range(GB):
                        pe.wait_ge(x2n_ok, b + 1)
                        x2T_tile(x2n0_sb[:, b, :], bank(O_BANK0 + b))
                wo_tile(g, 3, (0, 1) if hold else range(H))

            B_group(0, first=True)
            with pe.Fori(1, GROUPS - 2) as g:
                B_group(g)
            B_group(GROUPS - 2, hold=True)
            B_group(GROUPS - 1, last=True)

            def product(dst, whi, wlo, mhi, mlo, start, stop, short):
                if short == "moving lo is zero":
                    pe.matmul(dst, whi, mhi, start=start, stop=False)
                    return pe.matmul(dst, wlo, mhi, start=False, stop=stop)
                if short:
                    pe.matmul(dst, whi, mhi, start=start, stop=False)
                    return pe.matmul(dst, whi, mlo, start=False, stop=stop)
                return three(dst, whi, wlo, mhi, mlo, start, stop)

            def gate_up(g, c, first=None, short=False):
                n = CH * g + c
                if c == 0:
                    pe.wait_ge(x2l_ok, GB * (g + 1))
                if c >= 2:
                    pe.wait_ge(hdl_ok, n - 1)
                if first:
                    pe.wait_ge(wffn_ok, c + 1)
                    if c == 1:
                        pe.wait_ge(x2_ok, B)
                for j, done in ((0, gate_mm), (1, up_mm)):
                    for k in range(H):
                        cols = slice(j * D + k * P, j * D + (k + 1) * P)
                        mm = product(bank(GU_BANKS[c % 2][j]), chunk_w(c, 0)[:, cols], chunk_w(c, 1)[:, cols],
                                   x2h_sb[:, k, :, :].rearrange("p b s -> p (b s)"),
                                   x2l_sb[:, k, :, :].rearrange("p b s -> p (b s)"),
                                   start=(k == 0), stop=(k == H - 1), short=short)
                    mm.then_inc(done, 1)

            def down(g, c, short=False, token_tiles=range(GB)):
                if c == 0:
                    pe.wait_ge(sc_ok, GB * g)
                pe.wait_ge(hdl_ok, CH * g + c + 1)
                for b in token_tiles:
                    cols = slice(b * S, (b + 1) * S)
                    mm = product(bank(O_BANK0 + b), hd_sb[:, c % 2, 0, cols], hd_sb[:, c % 2, 1, cols],
                                 chunk_w(c, 0)[:, 2 * D:], chunk_w(c, 1)[:, 2 * D:],
                                 start=(c == 0), stop=(c == CH - 1),
                                 short="moving lo is zero" if short else False)
                    if c == CH - 1:
                        mm.then_inc(acc_mm, 1)
                if c < CH - 1 and token_tiles[-1] == GB - 1:
                    mm.then_inc(down_mm, 1)

            def C_end(g, last=False, short=False):
                if not last:
                    for b in (0, 1):
                        if b == 0:
                            pe.wait_ge(hdl_ok, CH * g + CH - 1)
                        pe.wait_ge(x2n_ok, GB * (g + 1) + b + 1)
                        x2T_tile(x2n_sb[:, b, :], bank(GU_BANKS[1][b]))
                else:
                    down(g, CH - 3, short, (2, 3))
                down(g, CH - 2, short)
                if not last:
                    for b in (2, 3):
                        if b == 2:
                            pe.wait_ge(hdl_ok, CH * g + CH)
                        pe.wait_ge(x2n_ok, GB * (g + 1) + b + 1)
                        x2T_tile(x2n_sb[:, b, :], bank(GU_BANKS[0][b - 2]))
                down(g, CH - 1, short)

            def C_step(g, c, first=False, last=False, short=False):
                gate_up(g, c, first, short)
                if last and c == CH - 2:
                    down(g, c - 1, short, (0, 1))
                elif 0 < c < CH - 1:
                    down(g, c - 1, short)

            def C_group(g, last=False, short=False):
                for c in range(CH):
                    C_step(g, c, last=last, short=short)
                C_end(g, last, short)

            def C_other_groups(short):
                with pe.Fori(1, GROUPS - 1) as g:
                    C_group(g, short=short)
                C_group(GROUPS - 1, last=True, short=short)

            for c in range(CH):
                pe.wait_ge(flag_ok, c + 1)
                some_lo = pe.value_load(flag[0:1, c:c + 1], min_val=0, max_val=1)
                with pe.If(some_lo != 0):
                    C_step(0, c, first=True)
                with pe.Else():
                    C_step(0, c, first=True, short=True)
            with pe.If(some_lo != 0):
                C_end(0)
                C_other_groups(short=False)
            with pe.Else():
                C_end(0, short=True)
                C_other_groups(short=True)

        @block.scalar
        def _(act):
            act.wait_ge(small_in, 16)
            nc.scalar.activation(tg[:], small[:, TG0:TG0 + 2], ACT.Tanh).then_inc(tanh_ok, 1)
            act.wait_ge(eps_ok, 2)
            nc.scalar.activation(std2[:, 0:2], eps[:], ACT.Sqrt).then_inc(table_ok, 1)
            for h in range(H):
                act.wait_ge(g_mm, h + 1)
                nc.scalar.activation(g_sb[:, h, :], bank(G_BANKS[h])[:, 0:P], ACT.Copy).then_inc(g_ok, 1)

            def w_hi(c, out, raw):
                act.wait_ge(wffn_in, 16 * (c + 1))
                nc.scalar.activation(out, raw, ACT.Copy).then_inc(wffn_hi, 1)

            def w_sum(c, lo, junk):
                if c:
                    act.wait_ge(losum_ok, c)
                act.wait_ge(wffn_ok, c + 1)
                nc.scalar.activation(junk[:], lo.bitcast(F32), ACT.Abs, accum_out=losum[:, c:c + 1]
                                     ).then_inc(losum_ok, 1)

            def std_group(n, eps_col):
                act.wait_ge(mv_ok, GB * (n + 1))
                act.wait_ge(rstd_ok, n)
                nc.scalar.activation(std[:], mv[:, :, 1], ACT.Sqrt, bias=eps[:, eps_col:eps_col + 1]
                                     ).then_inc(std_ok, 1)

            def v_hi_part(g):
                act.wait_ge(o_mm, g)
                for h in range(H):
                    nc.scalar.activation(v_hi[:, h], v_sb[:, h, tiles(g), :], ACT.Copy).then_inc(v_hi_ok, 1)

            def V_out(g, b):
                act.wait_ge(v_mm, GB * g + b + 1)
                src = bank(V_BANKS[b % 2]).rearrange("p (h e) -> p h e", h=H)
                nc.scalar.activation(v_sb[:, :, g * GB + b, :], src, ACT.Copy).then_inc(v_ok, 1)

            def xT_out(g, b):
                if b == 0:
                    act.wait_ge(w_mm, H * g)
                act.wait_ge(xt_mm, GB * g + b + 1)
                src = bank(X_BANKS[b]).rearrange("p (k s) -> p k s", k=H)
                nc.scalar.activation(xT_sb[:, :, b, :], src, ACT.Copy).then_inc(xt_full, 1)
                nc.scalar.activation(xTh_sb[:, :, b, :], src, ACT.Copy).then_inc(xt_hi, 1)

            def A_group(g, first=False, last=False):
                if not first:
                    act.wait_ge(s_mm, g)
                for h in range(H):
                    act.wait_ge(t_mm, H * g + h + 1)
                    nc.scalar.activation(t_sb[:, h, :], bank(T_BANKS[h % 2]), ACT.Copy).then_inc(t_ok, 1)
                if first:
                    V_out(g, 0)
                    std_group(0, 0)
                    for b in range(1, GB):
                        V_out(g, b)
                    for b in range(GB):
                        xT_out(g, b)
                else:
                    for b0 in (0, 2):
                        V_out(g, b0)
                        V_out(g, b0 + 1)
                        xT_out(g, b0)
                        xT_out(g, b0 + 1)
                if not last:
                    std_group(g + 1, 0)
                for e in range(H):
                    if last and e == 1:
                        act.wait_ge(a_ok, 1)
                        nc.scalar.activation(a_hi[:], aT_sb[:], ACT.Copy).then_inc(a_hi_ok, 1)
                        act.wait_ge(wo_in, 16)
                        for k in range(H):
                            nc.scalar.activation(wo_hi[:, k, :], wo_raw[:, k, :], ACT.Copy).then_inc(wo_hi_ok, 1)
                    if last and e == 2:
                        std_group(GROUPS, 1)
                        act.wait_ge(am_ok, 1)
                        v_hi_part(1)
                    act.wait_ge(w_mm, H * g + e + 1)
                    nc.scalar.activation(wT_sb[:, e, tokens(g)], bank(W_BANKS[e]), ACT.Relu
                                         ).then_inc(w_ok, 1)

            A_group(0, first=True)
            with act.Fori(1, GROUPS - 1) as g:
                A_group(g)
            A_group(GROUPS - 1, last=True)

            def y_block(g, k):
                act.wait_ge(zt_mm, H * g + k + 1)
                nc.scalar.activation(bank(Z_BANKS[k % 2]), bank(Z_BANKS[k % 2]), ACT.Identity,
                                     scale=small[:, GAM0 + k:GAM0 + k + 1],
                                     bias=small[:, BET0 + k:BET0 + k + 1]).then_inc(y_ok, 1)

            def wy_hi_block(g, k):
                act.wait_ge(wy_ok, H * g + k + 1)
                if g == GROUPS - 1:
                    act.wait_ge(*((wo_half, 1) if k < 2 else (wo_mm, GB * g)))
                elif k == 0:
                    act.wait_ge(wo_mm, GB * g)
                nc.scalar.activation(wy_hi[:, k, :, :].rearrange("p b s -> p (b s)"),
                                     bank(Z_BANKS[k % 2]), ACT.Copy).then_inc(wyh_ok, 1)

            def std2_tiles(first, n):
                act.wait_ge(mv2_ok, first + n)
                nc.scalar.activation(std2[:, first:first + n], l_mv[:, first:first + n, 1], ACT.Sqrt,
                                     bias=eps[:, 0:1]).then_inc(std2_ok, 1)

            def x2_hi(g, b, src):
                act.wait_ge(x2t_mm, GB * g + b + 1)
                nc.scalar.activation(x2h_sb[:, :, b, :], src.rearrange("p (k s) -> p k s", k=H), ACT.Copy
                                     ).then_inc(x2h_ok, 1)

            for g in range(GROUPS):
                y_block(g, 0)
                y_block(g, 1)
                wy_hi_block(g, 0)
                wy_hi_block(g, 1)
                y_block(g, 2)
                y_block(g, 3)
                wy_hi_block(g, 2)
                wy_hi_block(g, 3)
                if g + 2 < GROUPS:
                    v_hi_part(g + 2)
                w_hi(g, chunk_w(g, 0), chunk_raw(g))
                if g:
                    w_sum(g - 1, chunk_w(g - 1, 1), junk_B)
                if g < GROUPS - 1:
                    std_group(GROUPS + g + 1, 1)
            std2_tiles(0, GB)
            w_sum(AHEAD - 1, chunk_w(AHEAD - 1, 1), junk_B)
            for b in range(GB):
                x2_hi(0, b, bank(O_BANK0 + b))

            def C_group(g, first=False, last=False):
                for c in range(CH):
                    n = CH * g + c
                    if first and c == 4:
                        std2_tiles(GB, B - GB)
                    act.wait_ge(gate_mm, n + 1)
                    if c >= 2:
                        act.wait_ge(hd_ok, n - 1)
                    nc.scalar.activation(silu_sb[:, c % 2, :], bank(GU_BANKS[c % 2][0]), ACT.Silu,
                                         scale=small[:, GS0 + c:GS0 + c + 1]).then_inc(silu_ok, 1)
                    act.wait_ge(hd_ok, n + 1)
                    if c >= 2:
                        act.wait_ge(down_mm, (CH - 1) * g + c - 1)
                    elif c == 0:
                        act.wait_ge(acc_mm, GB * g)
                    nc.scalar.activation(hd_sb[:, c % 2, 0, :], bank(GU_BANKS[c % 2][1]), ACT.Copy
                                         ).then_inc(hdh_ok, 1)
                    if first and c + AHEAD < CH:
                        w_hi(c + AHEAD, chunk_w(c + AHEAD, 0), chunk_raw(c + AHEAD))
                    if first and 0 < c and c + AHEAD - 1 < CH:
                        w_sum(c + AHEAD - 1, chunk_w(c + AHEAD - 1, 1), junk_C)
                if not last:
                    for b in range(GB):
                        x2_hi(g + 1, b, bank(GU_BANKS[1 - b // 2][b % 2]))

            C_group(0, first=True)
            with act.Fori(1, GROUPS - 1) as g:
                C_group(g)
            C_group(GROUPS - 1, last=True)

        @block.vector
        def _(dve):
            nc.vector.memset(eps[:, 0:1], LN_EPS).then_inc(eps_ok, 1)
            nc.vector.memset(eps[:, 1:2], GN_EPS).then_inc(eps_ok, 1)

            def standing():
                nc.vector.memset(carrier[:], 0.0)

            def x_norm(g, first=False):
                if not first:
                    dve.wait_ge(x_in, 16 * g)
                    standing()
                for b in range(GB):
                    if first and b % 2 == 0:
                        dve.wait_ge(x0_in[b // 2], 16)
                    nc.vector.bn_stats(st6[:, b, :], x_sb[:, g * GB + b, :])
                dve.drain()
                for b in range(GB):
                    nc.vector.bn_aggr(mv[:, b, :], st6[:, b, :]).then_inc(mv_ok, 1)
                dve.wait_ge(std_ok, g + 1)
                nc.vector.reciprocal(rstd[:], std[:]).then_inc(rstd_ok, 1)
                dve.wait_ge(rstd_ok, g + 1)
                dve.wait_ge(xt_mm, GB * g)
                for b in range(GB):
                    nc.vector.tensor_scalar(z_sb[:, b, :], x_sb[:, g * GB + b, :], mv[:, b, 0:1],
                                            rstd[:, b:b + 1], ALU.subtract, ALU.mult).then_inc(xn_ok, 1)

            def xT_lo(g):
                for b in range(GB):
                    dve.wait_ge(xt_hi, GB * g + b + 1)
                    nc.vector.tensor_tensor(
                        xTl_sb[:, :, b, :], bank(X_BANKS[b]).rearrange("p (k s) -> p k s", k=H),
                        xTh_sb[:, :, b, :].bitcast(F32), ALU.subtract).then_inc(xt_lo, 1)

            x_norm(0, first=True)
            dve.wait_ge(wg_in, 16)
            for e in range(H):
                nc.vector.tensor_copy(wg_hi[:, e], wg_raw[:, e]).then_inc(wg_hi_ok, 1)
            dve.wait_ge(g_ok, H)
            nc.vector.tensor_copy(g_hi[:], g_sb[:]).then_inc(g_hi_ok, 1)
            with dve.Fori(0, GROUPS - 1) as g:
                xT_lo(g)
                x_norm(g + 1)
                dve.wait_ge(t_mm, H * (g + 1))
                dve.wait_ge(ctx_in, 16 * (g + 1))
                for h in range(H):
                    nc.vector.tensor_copy(ctx_hi[:, h], ctx_sb[:, h]).then_inc(ctx_hi_ok, 1)
            xT_lo(GROUPS - 1)

            dve.wait_ge(s_mm, GROUPS)
            dve.wait_ge(mask_in, 16)
            nc.vector.tensor_tensor(aT_sb[:].rearrange("p h s -> p (h s)"), bank(S_BANK),
                                    mask_sb[:].rearrange("p h s -> p (h s)"), ALU.mult).then_inc(am_ok, 1)
            dve.wait_ge(am_ok, 1)
            flat = aT_sb[:].rearrange("p h s -> p (h s)")
            nc.vector.scalar_tensor_tensor(flat, flat, -1.0, flat, ALU.mult, ALU.max).then_inc(am_ok, 1)
            dve.wait_ge(am_ok, 2)
            nc.vector.tensor_scalar(flat, flat, 1.0, None, ALU.max).then_inc(a_ok, 1)

            def O_stats(g, b):
                if b == 0:
                    dve.wait_ge(o_mm, g + 1)
                nc.vector.bn_stats(st6[:, b, :], ps[:, O_BANK0:O_BANK0 + H, b * P:(b + 1) * P])

            def O_mean():
                dve.drain()
                for b in range(GB):
                    nc.vector.bn_aggr(mv[:, b, :], st6[:, b, :]).then_inc(mv_ok, 1)

            def O_rstd(g):
                dve.wait_ge(std_ok, GROUPS + g + 1)
                nc.vector.reciprocal(rstd[:], std[:]).then_inc(rstd_ok, 1)
                dve.wait_ge(rstd_ok, GROUPS + g + 1)
                dve.wait_ge(zt_mm, H * g)

            def O_norm(b):
                nc.vector.tensor_scalar(z_sb[:, b, :].rearrange("p (h e) -> p h e", h=H),
                                        ps[:, O_BANK0:O_BANK0 + H, b * P:(b + 1) * P],
                                        mv[:, b, 0:1], rstd[:, b:b + 1], ALU.subtract, ALU.mult
                                        ).then_inc(z_ok, 1)

            def wy_mul(g, k):
                dve.wait_ge(y_ok, H * g + k + 1)
                nc.vector.tensor_tensor(bank(Z_BANKS[k % 2]), bank(Z_BANKS[k % 2]),
                                        wT_sb[:, k, tokens(g)], ALU.mult).then_inc(wy_ok, 1)

            def wy_lo_block(g, k):
                dve.wait_ge(wyh_ok, H * g + k + 1)
                nc.vector.tensor_tensor(wy_lo[:, k, :, :].rearrange("p b s -> p (b s)"),
                                        bank(Z_BANKS[k % 2]),
                                        wy_hi[:, k, :, :].rearrange("p b s -> p (b s)").bitcast(F32),
                                        ALU.subtract).then_inc(wyl_ok, 1)

            def residual(g, b):
                t = g * GB + b
                dve.wait_ge(wo_mm, t + 1)
                nc.vector.scalar_tensor_tensor(x_sb[:, t, :], bank(WO_BANKS[b % 2]), tg[:, 0:1],
                                               x_sb[:, t, :], ALU.mult, ALU.add).then_inc(x2_ok, 1)

            def x2_stats(g, b):
                if b == 0:
                    dve.wait_ge(x2_ok, GB * (g + 1))
                t = g * GB + b
                nc.vector.bn_stats(l_st6[:, t, :], x_sb[:, t, :])

            def x2_mean(g):
                dve.drain()
                for b in range(GB):
                    t = g * GB + b
                    nc.vector.bn_aggr(l_mv[:, t, :], l_st6[:, t, :]).then_inc(mv2_ok, 1)

            def x2_rstd(n, first, count):
                dve.wait_ge(std2_ok, n)
                nc.vector.reciprocal(rstd2[:, first:first + count], std2[:, first:first + count]
                                     ).then_inc(rstd2_ok, 1)

            def x2_norm(dst, g, b):
                t = g * GB + b
                nc.vector.tensor_scalar(dst[:, b, :], x_sb[:, t, :], l_mv[:, t, 0:1], rstd2[:, bass.ds(t, 1)],
                                        ALU.subtract, ALU.mult).then_inc(x2n_ok, 1)

            def x2_lo(g, b, src):
                dve.wait_ge(x2h_ok, GB * g + b + 1)
                nc.vector.tensor_tensor(x2l_sb[:, :, b, :], src.rearrange("p (k s) -> p k s", k=H),
                                        x2h_sb[:, :, b, :].bitcast(F32), ALU.subtract).then_inc(x2l_ok, 1)

            for b in range(GB):
                O_stats(0, b)
            O_mean()
            O_rstd(0)
            for b in range(GB):
                O_norm(b)
            dve.wait_ge(ds_in, 16)
            nc.vector.tensor_scalar(dsg_sb[:], dsg_sb[:], tg[:, 1:2], None, ALU.mult).then_inc(dsg_ok, 1)
            def B_group(g, first=False, last=False):
                if not first and not last:
                    residual(g - 1, 3)
                wy_mul(g, 0)
                wy_mul(g, 1)
                wy_lo_block(g, 0)
                wy_lo_block(g, 1)
                if last:
                    residual(g - 1, 3)

                def stats(b):
                    if last:
                        x2_stats(0, b)
                    else:
                        O_stats(g + 1, b)
                stats(0)
                stats(1)
                wy_mul(g, 2)
                wy_mul(g, 3)
                wy_lo_block(g, 2)
                wy_lo_block(g, 3)
                stats(2)
                stats(3)
                residual(g, 0)
                if last:
                    x2_mean(0)
                else:
                    O_mean()
                    residual(g, 1)
                    O_rstd(g + 1)
                    for b in range(GB):
                        O_norm(b)
                    residual(g, 2)

            B_group(0, first=True)
            with dve.Fori(1, GROUPS - 1) as g:
                B_group(g)
            B_group(GROUPS - 1, last=True)
            x2_rstd(1, 0, GB)
            dve.wait_ge(rstd2_ok, 1)
            x2_norm(x2n0_sb, 0, 0)
            x2_norm(x2n0_sb, 0, 1)
            residual(GROUPS - 1, 1)
            x2_norm(x2n0_sb, 0, 2)
            x2_norm(x2n0_sb, 0, 3)
            residual(GROUPS - 1, 2)
            for b in range(GB):
                x2_lo(0, b, bank(O_BANK0 + b))
            residual(GROUPS - 1, 3)

            def C_group(g, first=False, last=False):
                for c in range(CH):
                    n = CH * g + c
                    dve.wait_ge(silu_ok, n + 1)
                    dve.wait_ge(up_mm, n + 1)
                    u = bank(GU_BANKS[c % 2][1])
                    nc.vector.scalar_tensor_tensor(u, u, small[:, US0 + c:US0 + c + 1], silu_sb[:, c % 2, :],
                                                   ALU.mult, ALU.mult).then_inc(hd_ok, 1)
                    dve.wait_ge(hdh_ok, n + 1)
                    nc.vector.tensor_tensor(hd_sb[:, c % 2, 1, :], u, hd_sb[:, c % 2, 0, :].bitcast(F32),
                                            ALU.subtract).then_inc(hdl_ok, 1)
                    if first and 1 <= c < GROUPS:
                        for b in range(GB):
                            x2_stats(c, b)
                        x2_mean(c)
                    if first and c == GROUPS:
                        x2_rstd(2, GB, B - GB)
                    if not last and c in (8, 9):
                        if c == 8:
                            dve.wait_ge(x2t_mm, GB * (g + 1))
                            dve.wait_ge(rstd2_ok, 2)
                            if not first:
                                dve.wait_ge(fin_ok, GB * g)
                            if first:
                                dve.wait_ge(losum_ok, CH)
                        x2_norm(x2n_sb, g + 1, 2 * (c - 8))
                        x2_norm(x2n_sb, g + 1, 2 * (c - 8) + 1)
                if not last:
                    for b in range(GB):
                        x2_lo(g + 1, b, bank(GU_BANKS[1 - b // 2][b % 2]))
                def add_x2(b):
                    t = g * GB + b
                    dve.wait_ge(sc_ok, t + 1)
                    nc.vector.tensor_tensor(x_sb[:, t, :], sum_sb[:, b, :], x_sb[:, t, :], ALU.add
                                            ).then_inc(fin_dve, 1)

                for b in range(GB):
                    t = g * GB + b
                    if last and b == 2:
                        add_x2(0)
                    dve.wait_ge(acc_mm, t + 1)
                    if b == 0 and not last:
                        dve.wait_ge(x2t_mm, GB * (g + 2))
                    if b == 0 and last:
                        dve.wait_ge(fin_ok, GB * g)
                    nc.vector.tensor_tensor(sum_sb[:, b, :], bank(O_BANK0 + b), dsg_sb[:], ALU.mult
                                            ).then_inc(sc_ok, 1)
                if last:
                    add_x2(GB - 1)

            C_group(0, first=True)
            with dve.Fori(1, GROUPS - 1) as g:
                C_group(g)
            C_group(GROUPS - 1, last=True)


def decay_mask():
    gam = (1.0 - 2.0 ** (-5.0 - np.arange(H, dtype=np.float32))).astype(np.float32)
    idx = np.arange(S, dtype=np.float32)
    expo = idx[None, :] - idx[:, None]
    d = np.where(expo[None] <= 0, gam[:, None, None] ** expo[None], np.float32(0))
    d = d / np.sqrt(d.sum(axis=-1))[:, None, :] / np.sqrt(np.float32(P))
    return np.ascontiguousarray(d.transpose(2, 0, 1).astype(np.float32))


def kernel(**inputs):
    import concourse.bacc as bacc
    from concourse.bass_utils import run_bass_kernel_spmd

    a = {n: np.asarray(v) for n, v in inputs.items()}

    def rows(w):
        return w.reshape(-1, P, w.shape[-1]).transpose(1, 0, 2)

    def up_cols(w):
        return w.reshape(CH, P, H, P).transpose(0, 3, 2, 1).reshape(CH, P, D)

    Wh = a["L0_xattn_Wh"]
    data = {
        "x": a["x"],
        "ctxT": a["ctx_2048"].reshape(GROUPS, GB, S, H, P).transpose(0, 4, 3, 1, 2).reshape(GROUPS, P, H, NT),
        "WhT": Wh.transpose(2, 0, 1),
        "Wh": Wh.transpose(1, 0, 2),
        "wg": a["L0_xattn_wg_w"].reshape(H, P, H, P).transpose(1, 2, 0, 3),
        "wo": rows(a["L0_xattn_wo_w"]),
        "wffn": np.concatenate([up_cols(a["L0_ffn_gate_w"]), up_cols(a["L0_ffn_up_w"]),
                                a["L0_ffn_down_w"].T.reshape(CH, P, D)], axis=2),
        "smalls": np.concatenate(
            [a["L0_ffn_gate_s"].reshape(CH, P).T, a["L0_ffn_up_s"].reshape(CH, P).T,
             a["L0_xattn_gn_gamma"].reshape(H, P).T, a["L0_xattn_gn_beta"].reshape(H, P).T,
             np.broadcast_to(a["g_xattn"].reshape(1, 1), (P, 1)),
             np.broadcast_to(a["g_ffn"].reshape(1, 1), (P, 1))], axis=1),
        "down_s": a["L0_ffn_down_s"].reshape(1, D),
        "mask": decay_mask(),
    }
    nc = bacc.Bacc("TRN2", target_bir_lowering=False, num_devices=1)
    arrays, args = {}, []
    for name, v in data.items():
        v = np.ascontiguousarray(v)
        arrays[f"in_{name}"] = v
        args.append(nc.dram_tensor(f"in_{name}", v.shape, mybir.dt.from_np(v.dtype), kind="ExternalInput").ap())
    args.append(nc.dram_tensor("out_x", (B, S, D), F32, kind="ExternalOutput").ap())
    build(nc, *args)
    r = run_bass_kernel_spmd(nc, [arrays], core_ids=[0])
    return r.results[0]["out_x"]
```
